# Optimizing a Trainium2 kernel written in Bass

```python
import numpy as np
import jax
import jax.numpy as jnp

def _softmax(x, axis=-1):
    return jax.nn.softmax(x, axis=axis)

def _gelu(x):
    return jax.nn.gelu(x, approximate=True)

def _silu(x):
    return jax.nn.silu(x)

def _sigmoid(x):
    return jax.nn.sigmoid(x)

def _layernorm(x, axis=-1, eps=1e-05):
    m = jnp.mean(x, axis=axis, keepdims=True)
    v = jnp.var(x, axis=axis, keepdims=True)
    return (x - m) / jnp.sqrt(v + eps)

def _scatter_add(tgt, idx, src, axis=0):
    return tgt.at[idx].add(src)

def _segment_sum(src, seg, n):
    return jax.ops.segment_sum(src, seg, n)
kernel_name = 'mk_adaln_d1_jaxref_r8_ed65a6'

def setup_inputs(seed: int=0):
    np.random.seed(seed)
    _w = jnp.asarray

    def _L0_attn_setup():
        import jax, jax.numpy as jnp
        import numpy as np
        H = 512
        D = H // 4
        key = jax.random.key(seed)
        k1, k2, k3, k4, k5 = jax.random.split(key, 5)
        x = jax.random.normal(k1, (4, 512, H), dtype=jnp.float32)
        s_in = 1.0 / np.sqrt(H)
        Wqkv = jax.random.normal(k2, (H, 3 * D), dtype=jnp.float32) * s_in
        bqkv = jax.random.normal(k3, (3 * D,), dtype=jnp.float32) * 0.01
        Wo = jax.random.normal(k4, (D, H), dtype=jnp.float32) * (1.0 / np.sqrt(D))
        bo = jax.random.normal(k5, (H,), dtype=jnp.float32) * 0.01
        return {'x': x, 'Wqkv': Wqkv, 'bqkv': bqkv, 'Wo': Wo, 'bo': bo}
    _L0_attn_in = _L0_attn_setup()

    def _L0_ffn_setup():
        import jax, jax.numpy as jnp
        import numpy as np
        NUM_EXPERTS = 4
        HIDDEN = 512
        RANK = 8
        ALPHA = 8.0
        SCALE = ALPHA / RANK
        key = jax.random.key(seed)
        ks = jax.random.split(key, 6)
        B, T, H, E, R = (4, 512, HIDDEN, NUM_EXPERTS, RANK)
        x = jax.random.normal(ks[0], (B, T, H), dtype=jnp.float32)
        W_up = jax.random.normal(ks[1], (H, H), dtype=jnp.float32) / np.sqrt(H)
        gate_w = jax.random.normal(ks[2], (E, H), dtype=jnp.float32) / np.sqrt(H)
        expert_bias = jnp.zeros((E,), dtype=jnp.float32)
        lora_A = jax.random.normal(ks[3], (E, R, H), dtype=jnp.float32) / np.sqrt(H)
        lora_B = jax.random.normal(ks[4], (E, H, R), dtype=jnp.float32) * 0.01
        return {'x': x, 'W_up': W_up, 'gate_w': gate_w, 'expert_bias': expert_bias, 'lora_A': lora_A, 'lora_B': lora_B}
    _L0_ffn_in = _L0_ffn_setup()
    _L0_c = _w((lambda *s: np.random.randn(*s).astype(np.float32) * 0.05)(4, 512))
    _L0_wmod = _w((lambda *s: np.random.randn(*s).astype(np.float32) * 0.05)(512, 6 * 512) * 512 ** (-0.5))
    _d = {'L0_attn_x': _L0_attn_in['x'], 'L0_attn_Wqkv': _L0_attn_in['Wqkv'], 'L0_attn_bqkv': _L0_attn_in['bqkv'], 'L0_attn_Wo': _L0_attn_in['Wo'], 'L0_attn_bo': _L0_attn_in['bo'], 'L0_ffn_W_up': _L0_ffn_in['W_up'], 'L0_ffn_gate_w': _L0_ffn_in['gate_w'], 'L0_ffn_expert_bias': _L0_ffn_in['expert_bias'], 'L0_ffn_lora_A': _L0_ffn_in['lora_A'], 'L0_ffn_lora_B': _L0_ffn_in['lora_B'], 'L0_c': _L0_c, 'L0_wmod': _L0_wmod}
    _x0 = _d['L0_attn_x']
    _d['L0_attn_x'] = jax.random.normal(jax.random.fold_in(jax.random.key(seed), 1), (4, 512, 512), dtype=_x0.dtype)
    del _x0
    return _d

def reference(L0_attn_x, L0_attn_Wqkv, L0_attn_bqkv, L0_attn_Wo, L0_attn_bo, L0_ffn_W_up, L0_ffn_gate_w, L0_ffn_expert_bias, L0_ffn_lora_A, L0_ffn_lora_B, L0_c, L0_wmod):

    def _L0_attn_ref(x, Wqkv, bqkv, Wo, bo):
        import jax, jax.numpy as jnp
        import numpy as np
        H = 512
        D = H // 4
        B, S, C = x.shape
        d = C // 4
        qkv = jnp.einsum('bsc,cf->bsf', x, Wqkv) + bqkv
        qkv = qkv.reshape(B, S, 3, d)
        q, k, v = (qkv[:, :, 0], qkv[:, :, 1], qkv[:, :, 2])
        scale = 1.0 / jnp.sqrt(jnp.float32(d)).astype(x.dtype)
        attn = jnp.einsum('bqd,bkd->bqk', q, k) * scale
        attn = jax.nn.softmax(attn, axis=-1)
        out = jnp.einsum('bqk,bkd->bqd', attn, v)
        return jnp.einsum('bqd,dc->bqc', out, Wo) + bo

    def _L0_ffn_ref(x, W_up, gate_w, expert_bias, lora_A, lora_B):
        import jax, jax.numpy as jnp
        import numpy as np
        NUM_EXPERTS = 4
        HIDDEN = 512
        RANK = 8
        ALPHA = 8.0
        SCALE = ALPHA / RANK
        B, T, H = x.shape
        E = gate_w.shape[0]
        x_flat = x.reshape(-1, H)
        logits = x_flat @ gate_w.T + expert_bias
        top1 = jnp.argmax(logits, axis=-1)
        one_hot = jax.nn.one_hot(top1, E, dtype=x_flat.dtype)
        base_out = jnp.einsum('bth,oh->bto', x, W_up)
        z = jnp.einsum('nh,erh->ner', x_flat, lora_A)
        d = jnp.einsum('ner,ehr->neh', z, lora_B) * SCALE
        delta = jnp.einsum('neh,ne->nh', d, one_hot)
        return base_out + delta.reshape(B, T, H)
    x = L0_attn_x
    mod = (_silu(L0_c) @ L0_wmod).reshape(L0_c.shape[0], 6, 1, -1)
    sa, ca, ga, sb, cb, gb = (mod[:, 0], mod[:, 1], mod[:, 2], mod[:, 3], mod[:, 4], mod[:, 5])
    ga = (2 * (ga >= 0) - 1) * jnp.maximum(jnp.abs(ga), 0.25)
    gb = (2 * (gb >= 0) - 1) * jnp.maximum(jnp.abs(gb), 0.25)
    h = _layernorm(x, axis=-1) * (1 + ca) + sa
    x = x + ga * _L0_attn_ref(h, L0_attn_Wqkv, L0_attn_bqkv, L0_attn_Wo, L0_attn_bo)
    h = _layernorm(x, axis=-1) * (1 + cb) + sb
    x = x + gb * _L0_ffn_ref(h, L0_ffn_W_up, L0_ffn_gate_w, L0_ffn_expert_bias, L0_ffn_lora_A, L0_ffn_lora_B)
    return x

_drawn_inputs = setup_inputs


def setup_inputs(seed=0):
    import zlib

    import numpy as np

    out = dict(_drawn_inputs(seed))
    spreads = {'L0_ffn_expert_bias': (0.0, 0.8)}
    factors = {'L0_attn_Wqkv': 2.671,
     'L0_attn_bqkv': 8.0,
     'L0_attn_Wo': 2.689,
     'L0_attn_bo': 8.0,
     'L0_ffn_gate_w': 8.0,
     'L0_ffn_lora_A': 8.0,
     'L0_ffn_lora_B': 8.0}
    for name, (base, spread) in spreads.items():
        noise = np.random.default_rng([zlib.crc32(name.encode()), seed]).standard_normal(out[name].shape)
        drawn = base * np.exp(spread * noise) if base else spread * noise
        out[name] = jnp.asarray(drawn.astype(out[name].dtype))
    for name, factor in factors.items():
        out[name] = (out[name] * factor).astype(out[name].dtype)
    return out
```

```python
from contextlib import ExitStack

import concourse.bass as bass
from concourse import mybir

ALU = mybir.AluOpType
ACT = mybir.ActivationFunctionType
AX_X = mybir.AxisListType.X
F32 = mybir.dt.float32
F32R = mybir.dt.float32r

P = 128
B = 4
T = 512
H = 512
D = 128
E = 4
R = 8
NT = T // P
NK = H // P
ER = E * R
GZ = E + ER
LN_EPS = 1e-5
SCORE_SCALE = float(D) ** -0.5
GATE_FLOOR = 0.25
MOD_ORDER = ("sa", "ca", "ga", "gb", "sb", "cb")
MODT = ("sa", "ca", "sb", "cb")
GATE_STEPS = 4
Z_STEPS = 8


def psum_plan():
    order = [("tp", "cT"), ("mm", "mod", "sa"), ("mm", "mod", "ca")]

    def stage_a(b):
        return [("tp", "x1T", b, kt) for kt in range(NK)] + [("mm", "qkv", b, j) for j in range(3)]

    order += stage_a(0) + [("tp", "V", 0), ("tp", "gateA")]
    for b in range(B):
        order += [("mm", "S", b, t) for t in range(NT)]
        if b == 0:
            order += [("mm", "mod", s) for s in ("ga", "gb", "sb", "cb")] + [("tp", "loraB")]
            order += [("tp", "wupT", kt) for kt in range(NK)]
        else:
            order += [("tp", "gz", b - 1), ("ff", "F", b - 1, 0), ("tp", "zl", b - 1), ("ff", "F", b - 1, 1),
                      ("tp", "zT", b - 1)]
        order += [("tp", "PT", b, t) for t in range(NT)]
        order += [("ff", "F", b - 1, 2)] * (b > 0) + [("mm", "O", b)] + [("ff", "F", b - 1, 3)] * (b > 0)
        order += [("mm", "Y", b, t) for t in range(NT)]
        if b + 1 < B:
            order += stage_a(b + 1)
        order += [("tp", "x2T", b, kt) for kt in range(NK)]
        if b + 1 < B:
            order += [("tp", "V", b + 1)]
    b = B - 1
    order += [("tp", "gz", b), ("ff", "F", b, 0), ("tp", "zl", b), ("ff", "F", b, 1), ("tp", "zT", b),
              ("ff", "F", b, 2), ("ff", "F", b, 3)]
    banks = {"mm": (0, 1, 2), "tp": (3, 4, 5), "ff": (6, 7)}
    place, earlier, taken, holds = {}, {}, dict.fromkeys(banks, 0), [None] * 8
    for ring, *name in order:
        bank = banks[ring][taken[ring] % len(banks[ring])]
        taken[ring] += 1
        place[tuple(name)] = bank
        earlier[tuple(name)] = holds[bank]
        holds[bank] = tuple(name)
    return place, earlier


def adaln_block(nc: bass.Bass, x, wqkv, bqkv, wo, bo, wup, gate_w, expert_bias, lora_a, lora_b, c, wmod, out):
    place, earlier = psum_plan()
    with ExitStack() as ctx:
        def sb(name, shape, dt=F32):
            return ctx.enter_context(nc.sbuf_tensor(name, shape, dt))

        def sem(name):
            return ctx.enter_context(nc.semaphore(name))

        bank = [ctx.enter_context(nc.psum_tensor(f"bank{i}", [P, 512], F32)) for i in range(8)]

        ident = sb("ident", [P, P])
        neg_half = sb("neg_half", [P, NT])
        first_wins = sb("first_wins", [P, NT, E])
        logit_bias = sb("logit_bias", [P, NT, GZ])
        c_row = sb("c_row", [B, H])
        siluT = sb("siluT", [P, NK, B])
        modT = {s: sb(f"modT_{s}", [P, NK, B]) for s in ("sa", "ca", "sb", "cb")}
        gate_tmp = sb("gate_tmp", [B, 3, H])
        silu_tmp = gate_tmp
        gates = sb("gates", [B, 2, H])
        ga_bc = sb("ga_bc", [P, 2, H])
        gb_bc = sb("gb_bc", [P, 2, H])
        bo_bc = sb("bo_bc", [P, H])
        gabo = sb("gabo", [P, H])
        bqkv_col = sb("bqkv_col", [P, 3])
        ga_rows = sb("ga_rows", [GZ, H])
        lora_b_raw = sb("lora_b_raw", [P, NK, ER])
        stage = [sb(f"stage{i}", [P, NK, H]) for i in range(3)]
        wqkv_hi = sb("wqkv_hi", [P, NK, 3 * D], F32R)
        wqkv_lo = sb("wqkv_lo", [P, NK, 3 * D], F32R)
        wup_hi = sb("wup_hi", [P, NK, H], F32R)
        wup_lo = sb("wup_lo", [P, NK, H], F32R)
        wo_raw = sb("wo_raw", [P, H])
        wo_ga = sb("wo_ga", [P, H])
        wo_hi = sb("wo_hi", [P, H], F32R)
        wo_lo = sb("wo_lo", [P, H], F32R)
        gzw = sb("gzw", [P, NK, 2, GZ], F32R)
        lbw = sb("lbw", [P, H], F32R)
        xs = sb("xs", [P, B, NT, H])
        xn1 = sb("xn1", [P, NT, H])
        xn2_p = sb("xn2_p", [P, NT, H])
        h_full = sb("h_full", [P, 2, T])
        ahi = sb("ahi", [P, NK, T], F32R)
        alo = sb("alo", [P, NK, T], F32R)
        h2hi = sb("h2hi", [P, NK, T], F32R)
        h2lo = sb("h2lo", [P, NK, T], F32R)
        qk_hi = sb("qk_hi", [P, 2, T], F32R)
        qk_lo = sb("qk_lo", [P, 2, T], F32R)
        vT = sb("vT", [P, T])
        v_hi = sb("v_hi", [P, NT, D], F32R)
        v_lo = sb("v_lo", [P, NT, D], F32R)
        o_hi = sb("o_hi", [P, T], F32R)
        o_lo = sb("o_lo", [P, T], F32R)
        gz = sb("gz", [2 * GZ, T])
        zl_tmp = sb("zl_tmp", [P, NT, GZ])
        zl = sb("zl", [P, NT, GZ])
        z_arg = sb("z_arg", [P, 3, NT, E])
        z_max = sb("z_max", [P, 2, NT])
        zm = sb("zm", [P, NT, ER])
        zst = sb("zst", [P, NT, 2, 2, ER], F32R)
        zT = sb("zT", [P, T], F32R)
        f_gb = sb("f_gb", [P, 2, H])
        lora_b_rep = f_gb[:, 0, :].rearrange("p (k a z) -> p k a z", k=NK, a=4)
        lb_hi = h2lo[:, 0, :]
        stats = sb("stats", [P, 2, NT, 6])
        moments = sb("moments", [P, 2, NT, 2])
        var_eps = sb("var_eps", [P, 2, NT])
        rstd = sb("rstd", [P, 2, NT])
        row_max = sb("row_max", [P, NT])
        neg_max = sb("neg_max", [P, NT])
        row_sum = sb("row_sum", [P, NT])
        row_inv = sb("row_inv", [P, NT])

        c_in, wqkv_in, small_in, wo_in, ga_rows_in, lora_b_in = map(
            sem, ("c_in", "wqkv_in", "small_in", "wo_in", "ga_rows_in", "lora_b_in"))
        bo_in, eb_in = sem("bo_in"), sem("eb_in")
        wup_in = sem("wup_in")
        mod_in = {s: sem(f"mod_in_{s}") for s in ("sa", "ca", "ga", "gb", "sb", "cb")}
        x0_in = [sem(f"x0_in{t}") for t in range(NT)]
        x_in = [sem(f"x_in{b}") for b in range(B)]
        ga_bc_in = [sem(f"ga_bc_in{i}") for i in range(2)]
        gb_bc_in = [sem(f"gb_bc_in{i}") for i in range(2)]
        gates_out = sem("gates_out")
        stored = sem("stored")
        names = """const_ready dve_const silu_step siluT_psum siluT_ready mod_psum modT_ready gate_step gates_ready
            wqkv_hi_ready wqkv_lo_ready wup_hi_ready wup_lo_ready wo_ga_ready wo_hi_ready wo_lo_ready gabo_ready
            wupT_psum gateA_psum gzw_hi_ready gzw_lo_ready loraB_rep_ready loraB_psum lb_hi_ready lbw_ready
            ln1_stats ln1_aggr ln1_var ln1_rstd xn1_ready x1T_psum h1_full h1_hi h1_lo
            qkv_psum qk_hi_ready qk_lo_ready vT_ready V_psum v_hi_ready v_lo_ready
            S_psum max_ready negmax_ready p_ready PT_psum pt_hi pt_lo O_psum o_hi_ready o_lo_ready inv_ready
            Y_psum xb_ready x2_ready ln2_stats ln2_aggr ln2_var ln2_rstd xn2_ready x2T_psum h2_full h2_hi h2_lo
            gz_psum gz_ready zl_psum z_step zst_ready zT_psum zT_ready F_psum f_gb_ready out_ready""".split()
        S = {n: sem(n) for n in names}

        def at(*name):
            return bank[place[name]]

        def last_read(kind, *of):
            b, i = (*of, 0, 0)[:2] if kind != "mod" else (0, 0)
            return {
                "cT": ("siluT_ready", 1), "gateA": ("gzw_lo_ready", 1), "loraB": ("lbw_ready", 2),
                "wupT": ("wup_lo_ready", b + 1),
                "x1T": ("h1_full", NK * b + i + 1) if kind == "x1T" else None,
                "x2T": ("h2_full", NK * b + i + 1) if kind == "x2T" else None,
                "qkv": ("vT_ready", b + 1) if i == 2 else ("qk_lo_ready", 2 * b + i + 1),
                "V": ("v_lo_ready", b + 1), "S": ("p_ready", NT * b + i + 1), "PT": ("pt_lo", NT * b + i + 1),
                "O": ("o_lo_ready", b + 1), "Y": ("x2_ready", NT * b + i + 1),
                "gz": ("gz_ready", b + 1), "zl": ("z_step", Z_STEPS * b + 2), "zT": ("zT_ready", b + 1),
                "F": ("f_gb_ready", NT * b + i + 1),
                "mod": {"ga": ("gate_step", 1), "gb": ("gate_step", 1 + GATE_STEPS)}.get(
                    of[0] if of else "", ("modT_ready", MODT.index(of[0]) + 1 if of and of[0] in MODT else 0)),
            }[kind]

        gates_dram = nc.dram_tensor("gates_dram", (2, B, H), F32).ap()
        wmod_v = wmod.rearrange("(k p) (s n) -> s p k n", p=P, n=H)
        SECTION = {"sa": 0, "ca": 1, "ga": 2, "sb": 3, "cb": 4, "gb": 5}
        x_v = x.rearrange("b (t p) h -> b p t h", p=P)
        out_v = out.rearrange("b (t p) h -> b p t h", p=P)
        SLOT = {"wqkv": 0, "sa": 1, "ca": 2, "ga": 0, "gb": 1, "sb": 2, "cb": 0, "wup": 1}

        block = ctx.enter_context(nc.Block())

        @block.sync
        def _(sp):
            sp.dma_start(c_row[:], c).then_inc(c_in, 16)
            for t in range(NT):
                sp.dma_start(xs[:, 0, t, :], x_v[0, :, t, :]).then_inc(x0_in[t], 16)
            sp.dma_start(stage[SLOT["wqkv"]][:, :, 0:3 * D],
                         wqkv.rearrange("(k p) f -> p k f", p=P)).then_inc(wqkv_in, 16)
            for s in ("sa", "ca"):
                sp.dma_start(stage[SLOT[s]][:], wmod_v[SECTION[s]]).then_inc(mod_in[s], 16)
            sp.dma_start(bqkv_col[:], bqkv.rearrange("(j d) -> d j", d=D),
                         allow_slow_non_contiguous=True).then_inc(small_in, 16)
            sp.dma_start(wo_raw[:], wo).then_inc(wo_in, 16)
            sp.dma_start(bo_bc[:], bo.partition_broadcast(P)).then_inc(bo_in, 16)
            sp.dma_start(ga_rows[0:E, :], gate_w).then_inc(ga_rows_in, 16)
            sp.dma_start(ga_rows[E:GZ, :], lora_a.rearrange("e r h -> (e r) h")).then_inc(ga_rows_in, 16)
            sp.wait_ge(S["dve_const"], 2 + E)
            for t in range(NT):
                sp.dma_start(logit_bias[:, t, 0:E], expert_bias.partition_broadcast(P)).then_inc(eb_in, 16)
            for e in range(E):
                sp.dma_start(lora_b_raw[:, :, e * R:(e + 1) * R],
                             lora_b[e].rearrange("(k p) r -> p k r", p=P)).then_inc(lora_b_in, 16)
            sp.wait_ge(S["wqkv_hi_ready"], 1)
            sp.wait_ge(S["wqkv_lo_ready"], 1)
            sp.dma_start(stage[SLOT["ga"]][:], wmod_v[SECTION["ga"]]).then_inc(mod_in["ga"], 16)
            sp.wait_ge(S["mod_psum"], 1)
            sp.dma_start(stage[SLOT["gb"]][:], wmod_v[SECTION["gb"]]).then_inc(mod_in["gb"], 16)
            sp.wait_ge(S["mod_psum"], 2)
            sp.dma_start(stage[SLOT["sb"]][:], wmod_v[SECTION["sb"]]).then_inc(mod_in["sb"], 16)
            sp.dma_start(xs[:, 1], x_v[1]).then_inc(x_in[1], 16)
            sp.wait_ge(S["mod_psum"], 3)
            sp.dma_start(stage[SLOT["cb"]][:], wmod_v[SECTION["cb"]]).then_inc(mod_in["cb"], 16)
            sp.wait_ge(S["mod_psum"], 4)
            sp.dma_start(stage[SLOT["wup"]][:], wup.rearrange("(o p) h -> p o h", p=P)).then_inc(wup_in, 16)

            def write_gate(i):
                sp.wait_ge(S["gates_ready"], i + 1)
                sp.dma_start(gates_dram[i], gates[:, i, :]).then_inc(gates_out, 16)
                sp.wait_ge(gates_out, 16 * (i + 1))

            def spread_gates(b):
                if b >= 2:
                    sp.wait_ge(S["wo_ga_ready"], b - 1)
                    sp.wait_ge(S["gabo_ready"], b - 1)
                    sp.wait_ge(S["f_gb_ready"], NT * (b - 1))
                sp.dma_start(ga_bc[:, b % 2, :], gates_dram[0, b].partition_broadcast(P)).then_inc(ga_bc_in[b % 2], 16)
                if b == 0:
                    write_gate(1)
                sp.dma_start(gb_bc[:, b % 2, :], gates_dram[1, b].partition_broadcast(P)).then_inc(gb_bc_in[b % 2], 16)

            write_gate(0)
            spread_gates(0)
            spread_gates(1)
            for b in (2, 3):
                sp.dma_start(xs[:, b], x_v[b]).then_inc(x_in[b], 16)
            for b in range(B):
                if b >= 1 and b + 1 < B:
                    spread_gates(b + 1)
                for t in range(NT):
                    sp.wait_ge(S["out_ready"], NT * b + t + 1)
                    sp.dma_start(out_v[b, :, t, :], xs[:, b, t, :]).then_inc(stored, 16)
            sp.wait_ge(stored, 16 * B * NT)

        @block.tensor
        def _(pe):
            def open_bank(*name):
                before = earlier[name]
                if before is not None:
                    ready, count = last_read(*before)
                    pe.wait_ge(S[ready], count)
                return at(*name)

            def products(dst, pairs, n, first=True, last=True):
                total = 3 * len(pairs)
                i = 0
                for (w_hi, w_lo), (m_hi, m_lo) in pairs:
                    for w, m in ((w_hi, m_lo), (w_lo, m_hi), (w_hi, m_hi)):
                        mm = nc.tensor.matmul(dst, w, m, start=first and i == 0, stop=last and i == total - 1)
                        i += 1
                return mm

            def mod_columns(s):
                dst = open_bank("mod", s)
                pe.wait_ge(mod_in[s], 16)
                for ht in range(NK):
                    for kt in range(NK):
                        mm = nc.tensor.matmul(dst[:, B * ht:B * ht + B], stage[SLOT[s]][:, kt, ht * P:(ht + 1) * P],
                                              siluT[:, kt, :], start=kt == 0, stop=kt == NK - 1)
                mm.then_inc(S["mod_psum"], 1)

            def mod_rows(s):
                dst = open_bank("mod", s)
                pe.wait_ge(mod_in[s], 16)
                for kt in range(NK):
                    mm = nc.tensor.matmul(dst[0:B, :], siluT[:, kt, :], stage[SLOT[s]][:, kt, :],
                                          start=kt == 0, stop=kt == NK - 1)
                mm.then_inc(S["mod_psum"], 1)

            def x1_transposes(b):
                pe.wait_ge(S["xn1_ready"], NT * (b + 1))
                for kt in range(NK):
                    dst = open_bank("x1T", b, kt)
                    for t in range(NT):
                        mm = nc.tensor.transpose(dst[:, t * P:(t + 1) * P], xn1[:, t, kt * P:(kt + 1) * P], ident[:])
                    mm.then_inc(S["x1T_psum"], 1)

            def qkv(b):
                dst = [open_bank("qkv", b, j) for j in range(3)]
                if b == 0:
                    pe.wait_ge(S["wqkv_hi_ready"], 1)
                    pe.wait_ge(S["wqkv_lo_ready"], 1)
                for kt in range(NK):
                    pe.wait_ge(S["h1_hi"], NK * b + kt + 1)
                    pe.wait_ge(S["h1_lo"], NK * b + kt + 1)
                    for j in range(3):
                        f = slice(j * D, (j + 1) * D)
                        mm = products(dst[j][:], [((wqkv_hi[:, kt, f], wqkv_lo[:, kt, f]), (ahi[:, kt, :], alo[:, kt, :]))],
                                      T, first=kt == 0, last=kt == NK - 1)
                        if kt == NK - 1:
                            mm.then_inc(S["qkv_psum"], 1)

            def v_transposes(b):
                dst = open_bank("V", b)
                pe.wait_ge(S["vT_ready"], b + 1)
                for t in range(NT):
                    mm = nc.tensor.transpose(dst[:, t * D:(t + 1) * D], vT[:, t * P:(t + 1) * P], ident[:])
                mm.then_inc(S["V_psum"], 1)

            def scores(b):
                pe.wait_ge(S["qk_hi_ready"], 2 * (b + 1))
                pe.wait_ge(S["qk_lo_ready"], 2 * (b + 1))
                for t in range(NT):
                    dst = open_bank("S", b, t)
                    q = slice(t * P, (t + 1) * P)
                    products(dst[:], [((qk_hi[:, 0, q], qk_lo[:, 0, q]), (qk_hi[:, 1, :], qk_lo[:, 1, :]))],
                             T).then_inc(S["S_psum"], 1)

            def p_transposes(b):
                for t in range(NT):
                    dst = open_bank("PT", b, t)
                    pe.wait_ge(S["p_ready"], NT * b + t + 1)
                    for kt in range(NT):
                        mm = nc.tensor.transpose(dst[:, kt * P:(kt + 1) * P], xn2_p[:, t, kt * P:(kt + 1) * P], ident[:])
                    mm.then_inc(S["PT_psum"], 1)

            def pv(b):
                dst = open_bank("O", b)
                pe.wait_ge(S["v_hi_ready"], b + 1)
                pe.wait_ge(S["v_lo_ready"], b + 1)
                pe.wait_ge(S["pt_hi"], NT * (b + 1))
                pe.wait_ge(S["pt_lo"], NT * (b + 1))
                products(dst[:], [((v_hi[:, kt, :], v_lo[:, kt, :]), (ahi[:, kt, :], alo[:, kt, :])) for kt in range(NT)],
                         T).then_inc(S["O_psum"], 1)

            def out_projection(b):
                pe.wait_ge(S["wo_hi_ready"], b + 1)
                pe.wait_ge(S["wo_lo_ready"], b + 1)
                pe.wait_ge(S["o_hi_ready"], b + 1)
                pe.wait_ge(S["o_lo_ready"], b + 1)
                for t in range(NT):
                    dst = open_bank("Y", b, t)
                    q = slice(t * P, (t + 1) * P)
                    products(dst[:], [((o_hi[:, q], o_lo[:, q]), (wo_hi[:], wo_lo[:]))], H).then_inc(S["Y_psum"], 1)

            def x2_transposes(b):
                pe.wait_ge(S["xn2_ready"], NT * (b + 1))
                for kt in range(NK):
                    dst = open_bank("x2T", b, kt)
                    for t in range(NT):
                        mm = nc.tensor.transpose(dst[:, t * P:(t + 1) * P], xn2_p[:, t, kt * P:(kt + 1) * P], ident[:])
                    mm.then_inc(S["x2T_psum"], 1)

            def gate_and_lora_a(b):
                dst = open_bank("gz", b)
                if b == 0:
                    pe.wait_ge(S["gzw_hi_ready"], 1)
                    pe.wait_ge(S["gzw_lo_ready"], 1)
                for kt in range(NK):
                    pe.wait_ge(S["h2_hi"], NK * b + kt + 1)
                    pe.wait_ge(S["h2_lo"], NK * b + kt + 1)
                    w = gzw[:, kt, :, :].rearrange("p a g -> p (a g)")
                    nc.tensor.matmul(dst[0:2 * GZ, :], w, h2lo[:, kt, :], start=kt == 0, stop=False)
                    mm = nc.tensor.matmul(dst[0:2 * GZ, :], w, h2hi[:, kt, :], start=False, stop=kt == NK - 1)
                mm.then_inc(S["gz_psum"], 1)

            def up(b, t):
                dst = open_bank("F", b, t)
                if b == 0 and t == 0:
                    pe.wait_ge(S["wup_hi_ready"], NK)
                    pe.wait_ge(S["wup_lo_ready"], NK)
                q = slice(t * P, (t + 1) * P)
                products(dst[:], [((h2hi[:, kt, q], h2lo[:, kt, q]), (wup_hi[:, kt, :], wup_lo[:, kt, :]))
                                  for kt in range(NK)], H, last=False)

            def z_to_tokens(b):
                dst = open_bank("zl", b)
                pe.wait_ge(S["gz_ready"], b + 1)
                for t in range(NT):
                    mm = nc.tensor.transpose(dst[:, t * 2 * GZ:(t + 1) * 2 * GZ], gz[:, t * P:(t + 1) * P],
                                             ident[0:2 * GZ, 0:2 * GZ])
                mm.then_inc(S["zl_psum"], 1)

            def z_transposes(b):
                dst = open_bank("zT", b)
                pe.wait_ge(S["zst_ready"], 2 * (b + 1))
                for t in range(NT):
                    mm = nc.tensor.transpose(dst[:, t * P:(t + 1) * P],
                                             zst[:, t].bitcast(F32).rearrange("p a s z -> p (a s z)"), ident[:])
                mm.then_inc(S["zT_psum"], 1)

            def lora_up(b, t):
                if b == 0 and t == 0:
                    pe.wait_ge(S["lbw_ready"], 2)
                if t == 0:
                    pe.wait_ge(S["zT_ready"], b + 1)
                nc.tensor.matmul(at("F", b, t)[:], zT[:, t * P:(t + 1) * P], lbw[:], start=False,
                                 stop=True).then_inc(S["F_psum"], 1)

            pe.wait_ge(S["const_ready"], 2)
            dst = open_bank("cT")
            pe.wait_ge(S["silu_step"], 4)
            for kt in range(NK):
                mm = nc.tensor.transpose(dst[:, B * kt:B * kt + B], silu_tmp[:, 2, kt * P:(kt + 1) * P], ident[0:B, 0:B])
            mm.then_inc(S["siluT_psum"], 1)
            pe.wait_ge(S["siluT_ready"], 1)
            mod_columns("sa")
            mod_columns("ca")
            x1_transposes(0)
            qkv(0)
            v_transposes(0)
            dst = open_bank("gateA")
            pe.wait_ge(ga_rows_in, 32)
            for kt in range(NK):
                mm = nc.tensor.transpose(dst[:, kt * GZ:(kt + 1) * GZ], ga_rows[:, kt * P:(kt + 1) * P],
                                         ident[0:GZ, 0:GZ])
            mm.then_inc(S["gateA_psum"], 1)
            for b in range(B):
                scores(b)
                if b == 0:
                    mod_rows("ga")
                    mod_rows("gb")
                    mod_columns("sb")
                    mod_columns("cb")
                    dst = open_bank("loraB")
                    pe.wait_ge(S["loraB_rep_ready"], 4)
                    for kt in range(NK):
                        mm = nc.tensor.transpose(dst[:, kt * P:(kt + 1) * P],
                                                 lora_b_rep[:, kt].rearrange("p a z -> p (a z)"), ident[:])
                    mm.then_inc(S["loraB_psum"], 1)
                    pe.wait_ge(wup_in, 16)
                    for kt in range(NK):
                        dst = open_bank("wupT", kt)
                        for ot in range(NK):
                            mm = nc.tensor.transpose(dst[:, ot * P:(ot + 1) * P],
                                                     stage[SLOT["wup"]][:, ot, kt * P:(kt + 1) * P], ident[:])
                        mm.then_inc(S["wupT_psum"], 1)
                    p_transposes(b)
                    pv(b)
                else:
                    gate_and_lora_a(b - 1)
                    up(b - 1, 0)
                    z_to_tokens(b - 1)
                    up(b - 1, 1)
                    z_transposes(b - 1)
                    p_transposes(b)
                    lora_up(b - 1, 0)
                    lora_up(b - 1, 1)
                    up(b - 1, 2)
                    lora_up(b - 1, 2)
                    pv(b)
                    up(b - 1, 3)
                    lora_up(b - 1, 3)
                out_projection(b)
                if b + 1 < B:
                    x1_transposes(b + 1)
                    qkv(b + 1)
                x2_transposes(b)
                if b + 1 < B:
                    v_transposes(b + 1)
            b = B - 1
            gate_and_lora_a(b)
            up(b, 0)
            z_to_tokens(b)
            up(b, 1)
            z_transposes(b)
            for t in range(NT):
                if t >= 2:
                    up(b, t)
                lora_up(b, t)

        @block.scalar
        def _(act):
            def h1_evacuate(b):
                for kt in range(NK):
                    n = NK * b + kt
                    act.wait_ge(S["x1T_psum"], n + 1)
                    if b == 0 and kt == 0:
                        act.wait_ge(S["modT_ready"], 2)
                    if kt >= 2:
                        act.wait_ge(S["h1_lo"], n - 1)
                    elif b == 1:
                        act.wait_ge(S["h1_lo"], NK - 1 + kt)
                    elif b >= 2:
                        act.wait_ge(S["h2_lo"], NK * (b - 1) - 1 + kt)
                    nc.scalar.activation(h_full[:, n % 2, :], at("x1T", b, kt)[:], ACT.Identity,
                                         bias=modT["sa"][:, kt, b:b + 1], scale=modT["ca"][:, kt, b:b + 1]
                                         ).then_inc(S["h1_full"], 1)
                    act.wait_ge(S["h1_full"], n + 1)
                    if b and kt == 0:
                        act.wait_ge(S["O_psum"], b)
                    nc.scalar.activation(ahi[:, kt, :], h_full[:, n % 2, :], ACT.Copy).then_inc(S["h1_hi"], 1)

            def qkv_evacuate(b):
                for j in range(2):
                    act.wait_ge(S["qkv_psum"], 3 * b + j + 1)
                    if b:
                        act.wait_ge(S["S_psum"], NT * b)
                    if b == 0 and j == 0:
                        act.wait_ge(small_in, 16)
                    nc.scalar.activation(qk_hi[:, j, :], at("qkv", b, j)[:], ACT.Identity,
                                         bias=bqkv_col[:, j:j + 1]).then_inc(S["qk_hi_ready"], 1)
                act.wait_ge(S["qkv_psum"], 3 * b + 3)
                ins = nc.scalar.activation(vT[:], at("qkv", b, 2)[:], ACT.Identity, bias=bqkv_col[:, 2:3])
                ins.then_inc(S["vT_ready"], 1)

            def v_evacuate(b):
                act.wait_ge(S["V_psum"], b + 1)
                nc.scalar.activation(v_hi[:].rearrange("p t d -> p (t d)"), at("V", b)[:],
                                     ACT.Copy).then_inc(S["v_hi_ready"], 1)

            def softmax(b):
                for t in range(NT):
                    act.wait_ge(S["negmax_ready"], NT * b + t + 1)
                    if b and t == 0:
                        act.wait_ge(S["x2T_psum"], NK * b)
                    nc.scalar.activation(xn2_p[:, t, :], at("S", b, t)[:], ACT.Exp, bias=neg_max[:, t:t + 1],
                                         scale=SCORE_SCALE, accum_out=row_sum[:, t:t + 1]).then_inc(S["p_ready"], 1)

            def pt_hi(b):
                for t in range(NT):
                    act.wait_ge(S["PT_psum"], NT * b + t + 1)
                    nc.scalar.activation(ahi[:, :, t * P:(t + 1) * P],
                                         at("PT", b, t)[:].rearrange("p (k q) -> p k q", k=NT),
                                         ACT.Copy).then_inc(S["pt_hi"], 1)

            def h2_evacuate(b):
                for kt in range(NK):
                    n = NK * b + kt
                    act.wait_ge(S["x2T_psum"], n + 1)
                    if b == 0 and kt == 0:
                        act.wait_ge(S["modT_ready"], 4)
                    if kt >= 2:
                        act.wait_ge(S["h2_lo"], n - 1)
                    elif b + 1 < B:
                        act.wait_ge(S["h1_lo"], NK * (b + 2) - 1 + kt)
                    else:
                        act.wait_ge(S["h2_lo"], NK * b - 1 + kt)
                    nc.scalar.activation(h_full[:, n % 2, :], at("x2T", b, kt)[:], ACT.Identity,
                                         bias=modT["sb"][:, kt, b:b + 1], scale=modT["cb"][:, kt, b:b + 1]
                                         ).then_inc(S["h2_full"], 1)
                    act.wait_ge(S["h2_full"], n + 1)
                    if b and kt == 0:
                        act.wait_ge(S["F_psum"], NT * b)
                    nc.scalar.activation(h2hi[:, kt, :], h_full[:, n % 2, :], ACT.Copy).then_inc(S["h2_hi"], 1)

            def wo_split(b):
                act.wait_ge(S["wo_ga_ready"], b + 1)
                if b:
                    act.wait_ge(S["Y_psum"], NT * b)
                nc.scalar.activation(wo_hi[:], wo_ga[:], ACT.Copy).then_inc(S["wo_hi_ready"], 1)

            def gz_evacuate(b):
                act.wait_ge(S["gz_psum"], b + 1)
                if b:
                    act.wait_ge(S["zl_psum"], b)
                nc.scalar.activation(gz[:], at("gz", b)[0:2 * GZ, :], ACT.Copy).then_inc(S["gz_ready"], 1)

            def zT_evacuate(b):
                act.wait_ge(S["zT_psum"], b + 1)
                if b:
                    act.wait_ge(S["F_psum"], NT * b)
                nc.scalar.activation(zT[:], at("zT", b)[:], ACT.Copy).then_inc(S["zT_ready"], 1)

            act.wait_ge(c_in, 16)
            nc.scalar.activation(silu_tmp[:, 0, :], c_row[:], ACT.Exp, scale=-1.0).then_inc(S["silu_step"], 1)
            act.wait_ge(wqkv_in, 16)
            nc.scalar.activation(wqkv_hi[:], stage[SLOT["wqkv"]][:, :, 0:3 * D], ACT.Copy).then_inc(S["wqkv_hi_ready"], 1)
            h1_evacuate(0)
            qkv_evacuate(0)
            v_evacuate(0)
            act.wait_ge(S["gateA_psum"], 1)
            nc.scalar.activation(gzw[:, :, 0, :], at("gateA")[:, 0:NK * GZ].rearrange("p (k g) -> p k g", k=NK),
                                 ACT.Copy).then_inc(S["gzw_hi_ready"], 1)
            for b in range(B):
                softmax(b)
                if b == 0:
                    act.wait_ge(S["loraB_psum"], 1)
                    nc.scalar.activation(lb_hi, at("loraB")[:], ACT.Copy).then_inc(S["lb_hi_ready"], 1)
                    wo_split(0)
                    for kt in range(NK):
                        act.wait_ge(S["wupT_psum"], kt + 1)
                        nc.scalar.activation(wup_hi[:, kt, :], at("wupT", kt)[:], ACT.Copy).then_inc(S["wup_hi_ready"], 1)
                else:
                    gz_evacuate(b - 1)
                    wo_split(b)
                    zT_evacuate(b - 1)
                pt_hi(b)
                act.wait_ge(S["O_psum"], b + 1)
                nc.scalar.activation(o_hi[:], at("O", b)[:], ACT.Copy).then_inc(S["o_hi_ready"], 1)
                if b + 1 < B:
                    h1_evacuate(b + 1)
                    qkv_evacuate(b + 1)
                h2_evacuate(b)
                if b + 1 < B:
                    v_evacuate(b + 1)
            gz_evacuate(B - 1)
            zT_evacuate(B - 1)

        @block.vector
        def _(dve):
            def ln1_moments(b):
                for t in range(NT):
                    if b == 0:
                        dve.wait_ge(x0_in[t], 16)
                    elif t == 0:
                        dve.wait_ge(x_in[b], 16)
                        dve.wait_ge(S["xn1_ready"], NT * b)
                    nc.vector.bn_stats(stats[:, 0, t, :], xs[:, b, t, :]).then_inc(S["ln1_stats"], 1)
                for t in range(NT):
                    dve.wait_ge(S["ln1_stats"], NT * b + t + 1)
                    nc.vector.bn_aggr(moments[:, 0, t, :], stats[:, 0, t, :]).then_inc(S["ln1_aggr"], 1)
                dve.wait_ge(S["ln1_aggr"], NT * (b + 1))
                nc.vector.tensor_scalar(var_eps[:, 0, :], moments[:, 0, :, 1], LN_EPS, None,
                                        ALU.add).then_inc(S["ln1_var"], 1)

            def mod_evacuate(s):
                dve.wait_ge(S["mod_psum"], MOD_ORDER.index(s) + 1)
                nc.vector.tensor_scalar(modT[s][:].rearrange("p k b -> p (k b)"), at("mod", s)[:, 0:NK * B],
                                        1.0 if s in ("ca", "cb") else 0.0, None,
                                        ALU.add).then_inc(S["modT_ready"], 1)

            def gate_rows(i, s):
                done = GATE_STEPS * i
                dve.wait_ge(S["mod_psum"], MOD_ORDER.index(s) + 1)
                nc.vector.tensor_copy(gate_tmp[:, 2, :], at("mod", s)[0:B, :]).then_inc(S["gate_step"], 1)
                dve.wait_ge(S["gate_step"], done + 1)
                nc.vector.scalar_tensor_tensor(gate_tmp[:, 0, :], gate_tmp[:, 2, :], -1.0, gate_tmp[:, 2, :], ALU.mult,
                                               ALU.max).then_inc(S["gate_step"], 1)
                nc.vector.tensor_scalar(gate_tmp[:, 1, :], gate_tmp[:, 2, :], 0.0, 2.0, ALU.is_ge,
                                        ALU.mult).then_inc(S["gate_step"], 1)
                dve.wait_ge(S["gate_step"], done + 3)
                nc.vector.tensor_scalar(gate_tmp[:, 2, :], gate_tmp[:, 0, :], GATE_FLOOR, None,
                                        ALU.max).then_inc(S["gate_step"], 1)
                dve.wait_ge(S["gate_step"], done + 4)
                nc.vector.scalar_tensor_tensor(gates[:, i, :], gate_tmp[:, 1, :], -1.0, gate_tmp[:, 2, :], ALU.add,
                                               ALU.mult).then_inc(S["gates_ready"], 1)
                dve.wait_ge(S["gates_ready"], i + 1)

            def h1_low(b):
                for kt in range(NK):
                    n = NK * b + kt
                    dve.wait_ge(S["h1_hi"], n + 1)
                    nc.vector.tensor_tensor(alo[:, kt, :], h_full[:, kt % 2, :], ahi[:, kt, :].bitcast(F32),
                                            ALU.subtract).then_inc(S["h1_lo"], 1)

            def h2_low(b):
                for kt in range(NK):
                    n = NK * b + kt
                    dve.wait_ge(S["h2_hi"], n + 1)
                    nc.vector.tensor_tensor(h2lo[:, kt, :], h_full[:, kt % 2, :], h2hi[:, kt, :].bitcast(F32),
                                            ALU.subtract).then_inc(S["h2_lo"], 1)

            def qk_low(b):
                for j in range(2):
                    dve.wait_ge(S["qk_hi_ready"], 2 * b + j + 1)
                    nc.vector.scalar_tensor_tensor(qk_lo[:, j, :], at("qkv", b, j)[:], bqkv_col[:, j:j + 1],
                                                   qk_hi[:, j, :].bitcast(F32), ALU.add,
                                                   ALU.subtract).then_inc(S["qk_lo_ready"], 1)

            def v_low(b):
                dve.wait_ge(S["v_hi_ready"], b + 1)
                nc.vector.tensor_tensor(v_lo[:].rearrange("p t d -> p (t d)"), at("V", b)[:],
                                        v_hi[:].bitcast(F32).rearrange("p t d -> p (t d)"),
                                        ALU.subtract).then_inc(S["v_lo_ready"], 1)

            def maxima(b):
                for t in range(NT):
                    dve.wait_ge(S["S_psum"], NT * b + t + 1)
                    nc.vector.reduce_max(row_max[:, t:t + 1], at("S", b, t)[:], AX_X).then_inc(S["max_ready"], 1)
                    dve.wait_ge(S["max_ready"], NT * b + t + 1)
                    nc.vector.tensor_scalar(neg_max[:, t:t + 1], row_max[:, t:t + 1], -SCORE_SCALE, None,
                                            ALU.mult).then_inc(S["negmax_ready"], 1)

            def pt_low(b, t):
                dve.wait_ge(S["pt_hi"], NT * b + t + 1)
                q = slice(t * P, (t + 1) * P)
                nc.vector.tensor_tensor(alo[:, :, q], at("PT", b, t)[:].rearrange("p (k q) -> p k q", k=NT),
                                        ahi[:, :, q].bitcast(F32), ALU.subtract).then_inc(S["pt_lo"], 1)

            def inverse_sums(b):
                dve.wait_ge(S["p_ready"], NT * (b + 1))
                nc.vector.reciprocal(row_inv[:], row_sum[:]).then_inc(S["inv_ready"], 1)

            def o_low(b):
                dve.wait_ge(S["o_hi_ready"], b + 1)
                nc.vector.tensor_tensor(o_lo[:], at("O", b)[:], o_hi[:].bitcast(F32),
                                        ALU.subtract).then_inc(S["o_lo_ready"], 1)

            def attention_residual(b):
                dve.wait_ge(S["inv_ready"], b + 1)
                for t in range(NT + 1):
                    if t < NT:
                        dve.wait_ge(S["Y_psum"], NT * b + t + 1)
                        dve.wait_ge(S["xb_ready"], NT * b + t + 1)
                        nc.vector.scalar_tensor_tensor(xs[:, b, t, :], at("Y", b, t)[:], row_inv[:, t:t + 1],
                                                       xs[:, b, t, :], ALU.mult, ALU.add).then_inc(S["x2_ready"], 1)
                    if t >= 1:
                        u = t - 1
                        n = NT * b + u + 1
                        dve.wait_ge(S["x2_ready"], n)
                        if b and u == 0:
                            dve.wait_ge(S["xn2_ready"], NT * b)
                        nc.vector.bn_stats(stats[:, 1, u, :], xs[:, b, u, :]).then_inc(S["ln2_stats"], 1)
                        dve.wait_ge(S["ln2_stats"], n)
                        nc.vector.bn_aggr(moments[:, 1, u, :], stats[:, 1, u, :]).then_inc(S["ln2_aggr"], 1)
                        dve.wait_ge(S["ln2_aggr"], n)
                        nc.vector.tensor_scalar(var_eps[:, 1, u:u + 1], moments[:, 1, u, 1:2], LN_EPS, None,
                                                ALU.add).then_inc(S["ln2_var"], 1)

            def choose_expert(b):
                parts = at("zl", b)[:, 0:NT * 2 * GZ].rearrange("p (t a g) -> p t a g", t=NT, a=2)
                done = Z_STEPS * b
                dve.wait_ge(S["zl_psum"], b + 1)
                if b == 0:
                    dve.wait_ge(eb_in, 16 * NT)
                nc.vector.tensor_tensor(zl_tmp[:], parts[:, :, 1, :], logit_bias[:], ALU.add).then_inc(S["z_step"], 1)
                dve.wait_ge(S["z_step"], done + 1)
                nc.vector.tensor_tensor(zl[:], parts[:, :, 0, :], zl_tmp[:], ALU.add).then_inc(S["z_step"], 1)
                dve.wait_ge(S["z_step"], done + 2)
                nc.vector.reduce_max(z_max[:, 0, :], zl[:, :, 0:E], AX_X).then_inc(S["z_step"], 1)
                dve.wait_ge(S["z_step"], done + 3)
                nc.vector.tensor_tensor(z_arg[:, 0], zl[:, :, 0:E], z_max[:, 0, :].unsqueeze(2).to_broadcast([P, NT, E]),
                                        ALU.is_equal).then_inc(S["z_step"], 1)
                dve.wait_ge(S["z_step"], done + 4)
                nc.vector.tensor_tensor(z_arg[:, 1], z_arg[:, 0], first_wins[:], ALU.mult).then_inc(S["z_step"], 1)
                dve.wait_ge(S["z_step"], done + 5)
                nc.vector.reduce_max(z_max[:, 1, :], z_arg[:, 1], AX_X).then_inc(S["z_step"], 1)
                dve.wait_ge(S["z_step"], done + 6)
                nc.vector.tensor_tensor(z_arg[:, 2], z_arg[:, 1], z_max[:, 1, :].unsqueeze(2).to_broadcast([P, NT, E]),
                                        ALU.is_equal).then_inc(S["z_step"], 1)
                dve.wait_ge(S["z_step"], done + 7)
                nc.vector.tensor_tensor(zm[:].rearrange("p t (e r) -> p t e r", e=E),
                                        zl[:, :, E:GZ].rearrange("p t (e r) -> p t e r", e=E),
                                        z_arg[:, 2].unsqueeze(3).to_broadcast([P, NT, E, R]),
                                        ALU.mult).then_inc(S["z_step"], 1)
                dve.wait_ge(S["z_step"], done + 8)
                if b:
                    dve.wait_ge(S["zT_psum"], b)
                twice = zm[:].unsqueeze(2).to_broadcast([P, NT, 2, ER])
                nc.vector.tensor_copy(zst[:, :, :, 0, :], twice).then_inc(S["zst_ready"], 1)
                dve.wait_ge(S["zst_ready"], 2 * b + 1)
                nc.vector.tensor_tensor(zst[:, :, :, 1, :], twice, zst[:, :, :, 0, :].bitcast(F32),
                                        ALU.subtract).then_inc(S["zst_ready"], 1)

            def gate_ffn(b, t):
                n = NT * b + t
                dve.wait_ge(S["F_psum"], n + 1)
                if t == 0:
                    dve.wait_ge(gb_bc_in[b % 2], 16 * (b // 2 + 1))
                if n >= 2:
                    dve.wait_ge(S["out_ready"], n - 1)
                nc.vector.tensor_tensor(f_gb[:, n % 2, :], at("F", b, t)[:], gb_bc[:, b % 2, :],
                                        ALU.mult).then_inc(S["f_gb_ready"], 1)

            nc.vector.memset(neg_half[:], -0.5).then_inc(S["dve_const"], 1)
            for e in range(E):
                nc.vector.memset(first_wins[:, :, e], float(E - e)).then_inc(S["dve_const"], 1)
            nc.vector.memset(logit_bias[:], 0.0).then_inc(S["dve_const"], 1)
            dve.wait_ge(S["silu_step"], 1)
            nc.vector.tensor_scalar(silu_tmp[:, 1, :], silu_tmp[:, 0, :], 1.0, None, ALU.add).then_inc(S["silu_step"], 1)
            dve.wait_ge(S["silu_step"], 2)
            nc.vector.reciprocal(silu_tmp[:, 0, :], silu_tmp[:, 1, :]).then_inc(S["silu_step"], 1)
            dve.wait_ge(S["silu_step"], 3)
            dve.wait_ge(c_in, 16)
            nc.vector.tensor_tensor(silu_tmp[:, 2, :], c_row[:], silu_tmp[:, 0, :], ALU.mult).then_inc(S["silu_step"], 1)
            dve.wait_ge(S["siluT_psum"], 1)
            nc.vector.tensor_copy(siluT[:].rearrange("p k b -> p (k b)"), at("cT")[:, 0:NK * B]).then_inc(S["siluT_ready"], 1)
            ln1_moments(0)
            dve.wait_ge(S["wqkv_hi_ready"], 1)
            nc.vector.tensor_tensor(wqkv_lo[:], stage[SLOT["wqkv"]][:, :, 0:3 * D], wqkv_hi[:].bitcast(F32),
                                    ALU.subtract).then_inc(S["wqkv_lo_ready"], 1)
            mod_evacuate("sa")
            mod_evacuate("ca")
            h1_low(0)
            dve.wait_ge(small_in, 16)
            qk_low(0)
            v_low(0)
            dve.wait_ge(S["gzw_hi_ready"], 1)
            nc.vector.tensor_tensor(gzw[:, :, 1, :], at("gateA")[:, 0:NK * GZ].rearrange("p (k g) -> p k g", k=NK),
                                    gzw[:, :, 0, :].bitcast(F32), ALU.subtract).then_inc(S["gzw_lo_ready"], 1)
            for b in range(B):
                maxima(b)
                if b == 0:
                    gate_rows(0, "ga")
                    gate_rows(1, "gb")
                    dve.wait_ge(lora_b_in, 16 * E)
                    for a in range(4):
                        nc.vector.tensor_copy(lora_b_rep[:, :, a, :], lora_b_raw[:]).then_inc(S["loraB_rep_ready"], 1)
                    mod_evacuate("sb")
                    mod_evacuate("cb")
                    ln1_moments(1)
                    dve.wait_ge(S["lb_hi_ready"], 1)
                    nc.vector.tensor_copy(lbw[0:2 * ER, :], lb_hi[0:2 * ER, :].bitcast(F32)).then_inc(S["lbw_ready"], 1)
                    nc.vector.tensor_tensor(lbw[2 * ER:4 * ER, :], at("loraB")[2 * ER:4 * ER, :],
                                            lb_hi[2 * ER:4 * ER, :].bitcast(F32),
                                            ALU.subtract).then_inc(S["lbw_ready"], 1)
                    for kt in range(NK):
                        dve.wait_ge(S["wup_hi_ready"], kt + 1)
                        nc.vector.tensor_tensor(wup_lo[:, kt, :], at("wupT", kt)[:], wup_hi[:, kt, :].bitcast(F32),
                                                ALU.subtract).then_inc(S["wup_lo_ready"], 1)
                else:
                    choose_expert(b - 1)
                    if b + 1 < B:
                        ln1_moments(b + 1)
                for t in range(NT):
                    pt_low(b, t)
                    if b and t == 2:
                        gate_ffn(b - 1, 0)
                inverse_sums(b)
                if b:
                    gate_ffn(b - 1, 1)
                    gate_ffn(b - 1, 2)
                o_low(b)
                if b:
                    gate_ffn(b - 1, 3)
                attention_residual(b)
                if b + 1 < B:
                    h1_low(b + 1)
                    qk_low(b + 1)
                h2_low(b)
                if b + 1 < B:
                    v_low(b + 1)
            choose_expert(B - 1)
            for t in range(NT):
                gate_ffn(B - 1, t)

        @block.gpsimd
        def _(pool):
            def ln1_normalise(b):
                pool.wait_ge(S["ln1_var"], b + 1)
                if b == 0:
                    pool.wait_ge(S["dve_const"], 1)
                nc.gpsimd.tensor_tensor(rstd[:, 0, :], var_eps[:, 0, :], neg_half[:], ALU.pow).then_inc(S["ln1_rstd"], 1)
                pool.wait_ge(S["ln1_rstd"], b + 1)
                if b:
                    pool.wait_ge(S["x1T_psum"], NK * b)
                for t in range(NT):
                    nc.gpsimd.tensor_scalar(xn1[:, t, :], xs[:, b, t, :], moments[:, 0, t, 0:1], rstd[:, 0, t:t + 1],
                                            ALU.subtract, ALU.mult).then_inc(S["xn1_ready"], 1)

            def output_weights(b):
                pool.wait_ge(ga_bc_in[b % 2], 16 * (b // 2 + 1))
                if b == 0:
                    pool.wait_ge(wo_in, 16)
                    pool.wait_ge(bo_in, 16)
                else:
                    pool.wait_ge(S["wo_hi_ready"], b)
                    pool.wait_ge(S["wo_lo_ready"], b)
                nc.gpsimd.tensor_tensor(wo_ga[:], wo_raw[:], ga_bc[:, b % 2, :], ALU.mult).then_inc(S["wo_ga_ready"], 1)
                if b:
                    pool.wait_ge(S["xb_ready"], NT * b)
                nc.gpsimd.tensor_tensor(gabo[:], bo_bc[:], ga_bc[:, b % 2, :], ALU.mult).then_inc(S["gabo_ready"], 1)
                pool.wait_ge(S["wo_hi_ready"], b + 1)
                nc.gpsimd.tensor_tensor(wo_lo[:], wo_ga[:], wo_hi[:].bitcast(F32), ALU.subtract).then_inc(S["wo_lo_ready"], 1)
                pool.wait_ge(S["gabo_ready"], b + 1)
                pool.wait_ge(S["xn1_ready"], NT * (b + 1))
                for t in range(NT):
                    nc.gpsimd.tensor_tensor(xs[:, b, t, :], xs[:, b, t, :], gabo[:], ALU.add).then_inc(S["xb_ready"], 1)

            def ln2_normalise(b):
                for t in range(NT):
                    n = NT * b + t + 1
                    pool.wait_ge(S["ln2_var"], n)
                    nc.gpsimd.tensor_tensor(rstd[:, 1, t:t + 1], var_eps[:, 1, t:t + 1], neg_half[:, 0:1],
                                            ALU.pow).then_inc(S["ln2_rstd"], 1)
                    pool.wait_ge(S["ln2_rstd"], n)
                    nc.gpsimd.tensor_scalar(xn2_p[:, t, :], xs[:, b, t, :], moments[:, 1, t, 0:1], rstd[:, 1, t:t + 1],
                                            ALU.subtract, ALU.mult).then_inc(S["xn2_ready"], 1)

            def outputs(b, tiles):
                for t in tiles:
                    n = NT * b + t
                    pool.wait_ge(S["f_gb_ready"], n + 1)
                    nc.gpsimd.tensor_tensor(xs[:, b, t, :], xs[:, b, t, :], f_gb[:, n % 2, :], ALU.add).then_inc(S["out_ready"], 1)

            nc.gpsimd.memset(ident[:], 0.0).then_inc(S["const_ready"], 1)
            pool.wait_ge(S["const_ready"], 1)
            nc.gpsimd.affine_select(out=ident[:], in_=ident[:], compare_op=ALU.not_equal, fill=1.0, base=0,
                                    pattern=[[-1, P]], channel_multiplier=1).then_inc(S["const_ready"], 1)
            ln1_normalise(0)
            for b in range(B):
                output_weights(b)
                if b + 1 < B:
                    ln1_normalise(b + 1)
                if b:
                    outputs(b - 1, range(NT))
                ln2_normalise(b)
            outputs(B - 1, range(NT))


_INS = ["L0_attn_x", "L0_attn_Wqkv", "L0_attn_bqkv", "L0_attn_Wo", "L0_attn_bo", "L0_ffn_W_up", "L0_ffn_gate_w",
        "L0_ffn_expert_bias", "L0_ffn_lora_A", "L0_ffn_lora_B", "L0_c", "L0_wmod"]


def kernel(**inputs):
    import numpy as _np
    import concourse.bacc as _bacc
    from concourse.bass_utils import run_bass_kernel_spmd as _run

    nc = _bacc.Bacc("TRN2", target_bir_lowering=False, num_devices=1)
    arrays, args = {}, []
    for name in _INS:
        a = _np.ascontiguousarray(inputs[name])
        arrays[f"in_{name}_dram"] = a
        args.append(nc.dram_tensor(f"in_{name}_dram", a.shape, mybir.dt.from_np(a.dtype), kind="ExternalInput").ap())
    out = nc.dram_tensor("out_0_dram", (B, T, H), F32, kind="ExternalOutput").ap()
    adaln_block(nc, *args, out)
    r = _run(nc, [arrays], core_ids=[0])
    return r.results[0]["out_0_dram"]
```

```python
from contextlib import ExitStack

import concourse.bass as bass
from concourse import mybir

ALU = mybir.AluOpType
ACT = mybir.ActivationFunctionType
AX_X = mybir.AxisListType.X
F32 = mybir.dt.float32
F32R = mybir.dt.float32r

P = 128
B = 4
T = 512
H = 512
D = 128
E = 4
R = 8
NT = T // P
NK = H // P
ER = E * R
GZ = E + ER
LN_EPS = 1e-5
SCORE_SCALE = float(D) ** -0.5
GATE_FLOOR = 0.25
MOD_ORDER = ("sa", "ca", "ga", "gb", "sb", "cb")
MODT = ("sa", "ca", "sb", "cb")
GATE_STEPS = 4
Z_STEPS = 8


def psum_plan():
    order = [("tp", "cT"), ("mm", "mod", "sa"), ("mm", "mod", "ca"), ("tp", "modT", "sa"), ("tp", "modT", "ca")]

    def scores(b):
        return [("mm", "S", b, t) for t in range(NT - 1)] + [("tp", "S", b, NT - 1), ("tp", "V", b)]

    order += [("tp", "x1T", 0, kt) for kt in range(NK)] + [("mm", "qkv", 0, j) for j in range(3)]
    order += [("mm", "mod", "ga")] + scores(0) + [("tp", "gateA")]
    order += [("mm", "mod", s) for s in ("gb", "sb", "cb")] + [("tp", "modT", "sb"), ("tp", "loraB"), ("tp", "modT", "cb")]
    order += [("tp", "wupT", kt) for kt in range(NK)]
    for b in range(B):
        if b:
            order += [("ff", "gz", b - 1), ("ff", "F", b - 1, 0), ("tp", "zl", b - 1), ("ff", "F", b - 1, 1)]
        order += [("tp", "PT", b, 0), ("tp", "PT", b, 1)]
        if b:
            order += [("ff", "F", b - 1, 2), ("tp", "zT", b - 1)]
        order += [("tp", "PT", b, 2), ("tp", "PT", b, 3)]
        if b:
            order += [("ff", "F", b - 1, 3)]
        order += [("mm", "O", b)]
        if b + 1 < B:
            order += [("tp", "x1T", b + 1, kt) for kt in range(NK)]
        order += [("mm", "Y", b, t) for t in range(NT)]
        if b + 1 < B:
            order += [("mm", "qkv", b + 1, j) for j in range(3)]
        order += [("tp", "x2T", b, kt) for kt in range(NK)]
        if b + 1 < B:
            order += scores(b + 1)
    b = B - 1
    order += [("ff", "gz", b), ("ff", "F", b, 0), ("tp", "zl", b), ("ff", "F", b, 1), ("ff", "F", b, 2),
              ("tp", "zT", b), ("ff", "F", b, 3)]
    banks = {"mm": (0, 1, 2), "tp": (3, 4), "ff": (5, 6, 7)}
    place, earlier, taken, holds = {}, {}, dict.fromkeys(banks, 0), [None] * 8
    for ring, *name in order:
        bank = banks[ring][taken[ring] % len(banks[ring])]
        taken[ring] += 1
        place[tuple(name)] = bank
        earlier[tuple(name)] = holds[bank]
        holds[bank] = tuple(name)
    return place, earlier


def adaln_block(nc: bass.Bass, x, wqkv, bqkv, wo, bo, wup, gate_w, expert_bias, lora_a, lora_b, c, wmod, out):
    place, earlier = psum_plan()
    with ExitStack() as ctx:
        def sb(name, shape, dt=F32):
            return ctx.enter_context(nc.sbuf_tensor(name, shape, dt))

        def sem(name):
            return ctx.enter_context(nc.semaphore(name))

        bank = [ctx.enter_context(nc.psum_tensor(f"bank{i}", [P, 512], F32)) for i in range(8)]

        ident = sb("ident", [P, P])
        neg_half = sb("neg_half", [P, NT])
        first_wins = sb("first_wins", [P, NT, E])
        logit_bias = sb("logit_bias", [P, NT, GZ])
        c_row = sb("c_row", [B, H])
        siluT = sb("siluT", [P, NK * B])
        modT = {s: sb(f"modT_{s}", [P, NK, B]) for s in ("sa", "ca", "sb", "cb")}
        gate_tmp = sb("gate_tmp", [B, 3, H])
        silu_tmp = sb("silu_tmp", [P, 3, NK * B])
        mod_row = sb("mod_row", [B, 2, H])
        gates = sb("gates", [B, 2, H])
        ga_bc = sb("ga_bc", [P, 2, H])
        gb_bc = sb("gb_bc", [P, 2, H])
        bo_bc = sb("bo_bc", [P, H])
        gabo = sb("gabo", [P, H])
        bqkv_col = sb("bqkv_col", [P, 3])
        ga_rows = sb("ga_rows", [GZ, H])
        lora_b_raw = sb("lora_b_raw", [P, NK, ER])
        stage = [sb(f"stage{i}", [P, NK, H]) for i in range(3)]
        wqkv_hi = sb("wqkv_hi", [P, NK, 3 * D], F32R)
        wqkv_lo = sb("wqkv_lo", [P, NK, 3 * D], F32R)
        wup_hi = sb("wup_hi", [P, NK, H], F32R)
        wup_lo = sb("wup_lo", [P, NK, H], F32R)
        wo_raw = sb("wo_raw", [P, H])
        wo_ga = sb("wo_ga", [P, H])
        wo_hi = sb("wo_hi", [P, H], F32R)
        wo_lo = sb("wo_lo", [P, H], F32R)
        gzw = sb("gzw", [P, NK, 2, GZ], F32R)
        lbw = sb("lbw", [P, H], F32R)
        xs = sb("xs", [P, B, NT, H])
        xn1 = sb("xn1", [P, NT, H])
        xn2_p = sb("xn2_p", [P, NT, H])
        h1_full_at = [xn2_p] + [stage[0]] * (B - 1)
        h2_full_at = [stage[2]] * B
        ahi = sb("ahi", [P, NK, T], F32R)
        alo = sb("alo", [P, NK, T], F32R)
        h2hi = sb("h2hi", [P, NK, T], F32R)
        h2lo = sb("h2lo", [P, NK, T], F32R)
        qk_hi = sb("qk_hi", [P, 2, T], F32R)
        qk_lo = sb("qk_lo", [P, 2, T], F32R)
        vT = sb("vT", [P, T])
        v_hi = sb("v_hi", [P, NT, D], F32R)
        v_lo = sb("v_lo", [P, NT, D], F32R)
        o_hi = sb("o_hi", [P, T], F32R)
        o_lo = sb("o_lo", [P, T], F32R)
        gz = sb("gz", [2 * GZ, T])
        zl_tmp = sb("zl_tmp", [P, NT, GZ])
        zl = sb("zl", [P, NT, GZ])
        z_arg = sb("z_arg", [P, 3, NT, E])
        z_max = sb("z_max", [P, 2, NT])
        zm = sb("zm", [P, NT, ER])
        zst = sb("zst", [P, NT, 2, 2, ER], F32R)
        zT = sb("zT", [P, T], F32R)
        f_gb = sb("f_gb", [P, 2, H])
        lora_b_rep = f_gb[:, 0, :].rearrange("p (k a z) -> p k a z", k=NK, a=4)
        lb_hi = h2lo[:, 0, :]
        stats = sb("stats", [P, 2, NT, 6])
        moments = sb("moments", [P, 2, NT, 2])
        var_eps = sb("var_eps", [P, 2, NT])
        rstd = sb("rstd", [P, 2, NT])
        row_max = sb("row_max", [P, NT])
        neg_max = sb("neg_max", [P, NT])
        row_sum = sb("row_sum", [P, NT])
        row_inv = sb("row_inv", [P, NT])

        c_in, wqkv_in, small_in, wo_in, ga_rows_in, lora_b_in = map(
            sem, ("c_in", "wqkv_in", "small_in", "wo_in", "ga_rows_in", "lora_b_in"))
        bo_in, eb_in = sem("bo_in"), sem("eb_in")
        wup_in = sem("wup_in")
        mod_in = {s: sem(f"mod_in_{s}") for s in ("ga", "gb", "sb", "cb")}
        first_mod_in = {s: [sem(f"first_mod_in_{s}{kt}") for kt in range(NK)] for s in ("sa", "ca")}
        x0_in = [sem(f"x0_in{t}") for t in range(NT)]
        x_in = [sem(f"x_in{b}") for b in range(B)]
        ga_bc_in = [sem(f"ga_bc_in{i}") for i in range(2)]
        gb_bc_in = [sem(f"gb_bc_in{i}") for i in range(2)]
        gates_out = sem("gates_out")
        stored = sem("stored")
        names = """const_ready dve_const silu_step cT_psum mod_row_ready modT_psum siluT_ready mod_psum modT_ready gate_step gates_ready
            wqkv_hi_ready wqkv_lo_ready wup_hi_ready wup_lo_ready wo_ga_ready wo_hi_ready wo_lo_ready gabo_ready
            wupT_psum gateA_psum gzw_hi_ready gzw_lo_ready loraB_rep_ready loraB_psum lb_hi_ready lbw_ready
            ln1_stats ln1_aggr ln1_var ln1_rstd xn1_ready x1T_psum h1_full h1_hi h1_lo
            qkv_psum qk_hi_ready qk_lo_ready vT_ready V_psum v_hi_ready v_lo_ready
            S_psum max_ready negmax_ready p_ready PT_psum pt_hi pt_lo O_psum o_hi_ready o_lo_ready inv_ready
            Y_psum xb_ready x2_ready ln2_stats ln2_aggr ln2_var ln2_rstd xn2_ready x2T_psum h2_full h2_hi h2_lo
            gz_psum gz_ready zl_psum z_step zst_ready zT_psum zT_ready F_psum f_gb_ready out_ready""".split()
        S = {n: sem(n) for n in names}

        def at(*name):
            return bank[place[name]]

        def last_read(kind, *of):
            b, i = (*of, 0, 0)[:2] if kind not in ("mod", "modT") else (0, 0)
            return {
                "cT": ("siluT_ready", 1), "gateA": ("gzw_lo_ready", 1), "loraB": ("lbw_ready", 2),
                "wupT": ("wup_lo_ready", b + 1),
                "x1T": ("h1_full", NK * b + i + 1) if kind == "x1T" else None,
                "x2T": ("h2_full", NK * b + i + 1) if kind == "x2T" else None,
                "qkv": ("vT_ready", b + 1) if i == 2 else ("qk_lo_ready", 2 * b + i + 1),
                "V": ("v_lo_ready", b + 1), "S": ("p_ready", NT * b + i + 1), "PT": ("pt_lo", NT * b + i + 1),
                "O": ("o_lo_ready", b + 1), "Y": ("x2_ready", NT * b + i + 1),
                "gz": ("gz_ready", b + 1), "zl": ("z_step", Z_STEPS * b + 2), "zT": ("zT_ready", b + 1),
                "F": ("f_gb_ready", NT * b + i + 1),
                "mod": {"ga": ("gate_step", 1), "gb": ("gate_step", 1 + GATE_STEPS)}.get(
                    of[0] if of else "", ("mod_row_ready", MODT.index(of[0]) + 1 if of and of[0] in MODT else 0)),
                "modT": ("modT_ready", MODT.index(of[0]) + 1 if of and of[0] in MODT else 0),
            }[kind]

        gates_dram = nc.dram_tensor("gates_dram", (2, B, H), F32).ap()
        wmod_v = wmod.rearrange("(k p) (s n) -> s p k n", p=P, n=H)
        SECTION = {"sa": 0, "ca": 1, "ga": 2, "sb": 3, "cb": 4, "gb": 5}
        x_v = x.rearrange("b (t p) h -> b p t h", p=P)
        out_v = out.rearrange("b (t p) h -> b p t h", p=P)
        SLOT = {"wqkv": 0, "sa": 1, "ca": 2, "ga": 0, "gb": 1, "sb": 2, "cb": 0, "wup": 1}

        block = ctx.enter_context(nc.Block())

        @block.sync
        def _(sp):
            sp.dma_start(c_row[:], c).then_inc(c_in, 16)
            for t in range(NT):
                sp.dma_start(xs[:, 0, t, :], x_v[0, :, t, :]).then_inc(x0_in[t], 16)
            for s in ("sa", "ca"):
                for kt in range(NK):
                    sp.dma_start(stage[SLOT[s]][:, kt, :], wmod_v[SECTION[s]][:, kt, :]).then_inc(first_mod_in[s][kt], 16)
            sp.dma_start(stage[SLOT["wqkv"]][:, :, 0:3 * D],
                         wqkv.rearrange("(k p) f -> p k f", p=P)).then_inc(wqkv_in, 16)
            sp.dma_start(bqkv_col[:], bqkv.rearrange("(j d) -> d j", d=D),
                         allow_slow_non_contiguous=True).then_inc(small_in, 16)
            sp.dma_start(wo_raw[:], wo).then_inc(wo_in, 16)
            sp.dma_start(bo_bc[:], bo.partition_broadcast(P)).then_inc(bo_in, 16)
            sp.dma_start(ga_rows[0:E, :], gate_w).then_inc(ga_rows_in, 16)
            sp.dma_start(ga_rows[E:GZ, :], lora_a.rearrange("e r h -> (e r) h")).then_inc(ga_rows_in, 16)
            sp.wait_ge(S["dve_const"], 2 + E)
            for t in range(NT):
                sp.dma_start(logit_bias[:, t, 0:E], expert_bias.partition_broadcast(P)).then_inc(eb_in, 16)
            for e in range(E):
                sp.dma_start(lora_b_raw[:, :, e * R:(e + 1) * R],
                             lora_b[e].rearrange("(k p) r -> p k r", p=P)).then_inc(lora_b_in, 16)
            sp.wait_ge(S["wqkv_hi_ready"], 1)
            sp.wait_ge(S["wqkv_lo_ready"], 1)
            sp.dma_start(stage[SLOT["ga"]][:], wmod_v[SECTION["ga"]]).then_inc(mod_in["ga"], 16)
            sp.wait_ge(S["mod_psum"], 1)
            sp.dma_start(stage[SLOT["gb"]][:], wmod_v[SECTION["gb"]]).then_inc(mod_in["gb"], 16)
            sp.wait_ge(S["mod_psum"], 2)
            sp.dma_start(stage[SLOT["sb"]][:], wmod_v[SECTION["sb"]]).then_inc(mod_in["sb"], 16)
            sp.dma_start(xs[:, 1], x_v[1]).then_inc(x_in[1], 16)
            sp.wait_ge(S["mod_psum"], 3)
            sp.dma_start(stage[SLOT["cb"]][:], wmod_v[SECTION["cb"]]).then_inc(mod_in["cb"], 16)
            sp.wait_ge(S["mod_psum"], 4)
            sp.dma_start(stage[SLOT["wup"]][:], wup.rearrange("(o p) h -> p o h", p=P)).then_inc(wup_in, 16)

            def write_gate(i):
                sp.wait_ge(S["gates_ready"], i + 1)
                sp.dma_start(gates_dram[i], gates[:, i, :]).then_inc(gates_out, 16)
                sp.wait_ge(gates_out, 16 * (i + 1))

            def spread_gates(b):
                if b >= 2:
                    sp.wait_ge(S["wo_ga_ready"], b - 1)
                    sp.wait_ge(S["gabo_ready"], b - 1)
                    sp.wait_ge(S["f_gb_ready"], NT * (b - 1))
                sp.dma_start(ga_bc[:, b % 2, :], gates_dram[0, b].partition_broadcast(P)).then_inc(ga_bc_in[b % 2], 16)
                if b == 0:
                    write_gate(1)
                sp.dma_start(gb_bc[:, b % 2, :], gates_dram[1, b].partition_broadcast(P)).then_inc(gb_bc_in[b % 2], 16)

            write_gate(0)
            spread_gates(0)
            spread_gates(1)
            for b in (2, 3):
                sp.dma_start(xs[:, b], x_v[b]).then_inc(x_in[b], 16)
            for b in range(B):
                if b >= 1 and b + 1 < B:
                    spread_gates(b + 1)
                for t in range(NT):
                    sp.wait_ge(S["out_ready"], NT * b + t + 1)
                    sp.dma_start(out_v[b, :, t, :], xs[:, b, t, :]).then_inc(stored, 16)
            sp.wait_ge(stored, 16 * B * NT)

        @block.tensor
        def _(pe):
            def open_bank(*name):
                before = earlier[name]
                if before is not None:
                    ready, count = last_read(*before)
                    pe.wait_ge(S[ready], count)
                return at(*name)

            def products(dst, pairs, n, first=True, last=True):
                total = 3 * len(pairs)
                i = 0
                for (w_hi, w_lo), (m_hi, m_lo) in pairs:
                    for w, m in ((w_hi, m_lo), (w_lo, m_hi), (w_hi, m_hi)):
                        mm = nc.tensor.matmul(dst, w, m, start=first and i == 0, stop=last and i == total - 1)
                        i += 1
                return mm

            def mod_rows(s):
                dst = open_bank("mod", s)
                if s in mod_in:
                    pe.wait_ge(mod_in[s], 16)
                for kt in range(NK):
                    if s in first_mod_in:
                        pe.wait_ge(first_mod_in[s][kt], 16)
                    mm = nc.tensor.matmul(dst[0:B, :], siluT[:, kt * B:(kt + 1) * B], stage[SLOT[s]][:, kt, :],
                                          start=kt == 0, stop=kt == NK - 1)
                mm.then_inc(S["mod_psum"], 1)

            def mod_columns(s):
                n = MODT.index(s)
                dst = open_bank("modT", s)
                pe.wait_ge(S["mod_row_ready"], n + 1)
                for kt in range(NK):
                    mm = nc.tensor.transpose(dst[:, kt * B:(kt + 1) * B], mod_row[:, n % 2, kt * P:(kt + 1) * P],
                                             ident[0:B, 0:B])
                mm.then_inc(S["modT_psum"], 1)

            def x1_transposes(b):
                pe.wait_ge(S["xn1_ready"], NT * (b + 1))
                for kt in range(NK):
                    dst = open_bank("x1T", b, kt)
                    for t in range(NT):
                        mm = nc.tensor.transpose(dst[:, t * P:(t + 1) * P], xn1[:, t, kt * P:(kt + 1) * P], ident[:])
                    mm.then_inc(S["x1T_psum"], 1)

            def qkv(b, kts):
                if b == 0:
                    pe.wait_ge(S["wqkv_hi_ready"], 1)
                    pe.wait_ge(S["wqkv_lo_ready"], 1)
                for kt in kts:
                    pe.wait_ge(S["h1_hi"], NK * b + kt + 1)
                    pe.wait_ge(S["h1_lo"], NK * b + kt + 1)
                    for j in range(3):
                        f = slice(j * D, (j + 1) * D)
                        dst = open_bank("qkv", b, j) if kt == 0 else at("qkv", b, j)
                        mm = products(dst[:], [((wqkv_hi[:, kt, f], wqkv_lo[:, kt, f]), (ahi[:, kt, :], alo[:, kt, :]))],
                                      T, first=kt == 0, last=kt == NK - 1)
                        if kt == NK - 1:
                            mm.then_inc(S["qkv_psum"], 1)

            def v_transposes(b):
                dst = open_bank("V", b)
                pe.wait_ge(S["vT_ready"], b + 1)
                for t in range(NT):
                    mm = nc.tensor.transpose(dst[:, t * D:(t + 1) * D], vT[:, t * P:(t + 1) * P], ident[:])
                mm.then_inc(S["V_psum"], 1)

            def scores(b):
                pe.wait_ge(S["qk_hi_ready"], 2 * (b + 1))
                pe.wait_ge(S["qk_lo_ready"], 2 * (b + 1))
                for t in range(NT):
                    dst = open_bank("S", b, t)
                    q = slice(t * P, (t + 1) * P)
                    products(dst[:], [((qk_hi[:, 0, q], qk_lo[:, 0, q]), (qk_hi[:, 1, :], qk_lo[:, 1, :]))],
                             T).then_inc(S["S_psum"], 1)

            def p_transposes(b, tiles):
                for t in tiles:
                    dst = open_bank("PT", b, t)
                    pe.wait_ge(S["p_ready"], NT * b + t + 1)
                    for kt in range(NT):
                        mm = nc.tensor.transpose(dst[:, kt * P:(kt + 1) * P], xn2_p[:, t, kt * P:(kt + 1) * P], ident[:])
                    mm.then_inc(S["PT_psum"], 1)

            def pv(b):
                dst = open_bank("O", b)
                pe.wait_ge(S["v_hi_ready"], b + 1)
                pe.wait_ge(S["v_lo_ready"], b + 1)
                pe.wait_ge(S["pt_hi"], NT * (b + 1))
                pe.wait_ge(S["pt_lo"], NT * (b + 1))
                products(dst[:], [((v_hi[:, kt, :], v_lo[:, kt, :]), (ahi[:, kt, :], alo[:, kt, :])) for kt in range(NT)],
                         T).then_inc(S["O_psum"], 1)

            def out_projection(b):
                pe.wait_ge(S["wo_hi_ready"], b + 1)
                pe.wait_ge(S["wo_lo_ready"], b + 1)
                pe.wait_ge(S["o_hi_ready"], b + 1)
                pe.wait_ge(S["o_lo_ready"], b + 1)
                for t in range(NT):
                    dst = open_bank("Y", b, t)
                    q = slice(t * P, (t + 1) * P)
                    products(dst[:], [((o_hi[:, q], o_lo[:, q]), (wo_hi[:], wo_lo[:]))], H).then_inc(S["Y_psum"], 1)

            def x2_transposes(b):
                pe.wait_ge(S["xn2_ready"], NT * (b + 1))
                for kt in range(NK):
                    dst = open_bank("x2T", b, kt)
                    for t in range(NT):
                        mm = nc.tensor.transpose(dst[:, t * P:(t + 1) * P], xn2_p[:, t, kt * P:(kt + 1) * P], ident[:])
                    mm.then_inc(S["x2T_psum"], 1)

            def gate_and_lora_a(b):
                dst = open_bank("gz", b)
                if b == 0:
                    pe.wait_ge(S["gzw_hi_ready"], 1)
                    pe.wait_ge(S["gzw_lo_ready"], 1)
                for kt in range(NK):
                    pe.wait_ge(S["h2_hi"], NK * b + kt + 1)
                    pe.wait_ge(S["h2_lo"], NK * b + kt + 1)
                    w = gzw[:, kt, :, :].rearrange("p a g -> p (a g)")
                    nc.tensor.matmul(dst[0:2 * GZ, :], w, h2lo[:, kt, :], start=kt == 0, stop=False)
                    mm = nc.tensor.matmul(dst[0:2 * GZ, :], w, h2hi[:, kt, :], start=False, stop=kt == NK - 1)
                mm.then_inc(S["gz_psum"], 1)

            def up(b, t):
                dst = open_bank("F", b, t)
                if b == 0 and t == 0:
                    pe.wait_ge(S["wup_hi_ready"], NK)
                    pe.wait_ge(S["wup_lo_ready"], NK)
                q = slice(t * P, (t + 1) * P)
                products(dst[:], [((h2hi[:, kt, q], h2lo[:, kt, q]), (wup_hi[:, kt, :], wup_lo[:, kt, :]))
                                  for kt in range(NK)], H, last=False)

            def z_to_tokens(b):
                dst = open_bank("zl", b)
                pe.wait_ge(S["gz_ready"], b + 1)
                for t in range(NT):
                    mm = nc.tensor.transpose(dst[:, t * 2 * GZ:(t + 1) * 2 * GZ], gz[:, t * P:(t + 1) * P],
                                             ident[0:2 * GZ, 0:2 * GZ])
                mm.then_inc(S["zl_psum"], 1)

            def z_transposes(b):
                dst = open_bank("zT", b)
                pe.wait_ge(S["zst_ready"], 2 * (b + 1))
                for t in range(NT):
                    mm = nc.tensor.transpose(dst[:, t * P:(t + 1) * P],
                                             zst[:, t].bitcast(F32).rearrange("p a s z -> p (a s z)"), ident[:])
                mm.then_inc(S["zT_psum"], 1)

            def lora_up(b, t):
                if b == 0 and t == 0:
                    pe.wait_ge(S["lbw_ready"], 2)
                if t == 0:
                    pe.wait_ge(S["zT_ready"], b + 1)
                nc.tensor.matmul(at("F", b, t)[:], zT[:, t * P:(t + 1) * P], lbw[:], start=False,
                                 stop=True).then_inc(S["F_psum"], 1)

            pe.wait_ge(S["const_ready"], 2)
            dst = open_bank("cT")
            pe.wait_ge(c_in, 16)
            for kt in range(NK):
                mm = nc.tensor.transpose(dst[:, B * kt:B * kt + B], c_row[:, kt * P:(kt + 1) * P], ident[0:B, 0:B])
            mm.then_inc(S["cT_psum"], 1)
            pe.wait_ge(S["siluT_ready"], 1)
            mod_rows("sa")
            mod_rows("ca")
            mod_columns("sa")
            mod_columns("ca")
            x1_transposes(0)
            qkv(0, range(NK))
            mod_rows("ga")
            scores(0)
            v_transposes(0)
            dst = open_bank("gateA")
            pe.wait_ge(ga_rows_in, 32)
            for kt in range(NK):
                mm = nc.tensor.transpose(dst[:, kt * GZ:(kt + 1) * GZ], ga_rows[:, kt * P:(kt + 1) * P],
                                         ident[0:GZ, 0:GZ])
            mm.then_inc(S["gateA_psum"], 1)
            mod_rows("gb")
            mod_rows("sb")
            mod_rows("cb")
            mod_columns("sb")
            dst = open_bank("loraB")
            pe.wait_ge(S["loraB_rep_ready"], 4)
            for kt in range(NK):
                mm = nc.tensor.transpose(dst[:, kt * P:(kt + 1) * P],
                                         lora_b_rep[:, kt].rearrange("p a z -> p (a z)"), ident[:])
            mm.then_inc(S["loraB_psum"], 1)
            mod_columns("cb")
            pe.wait_ge(wup_in, 16)
            for kt in range(NK):
                dst = open_bank("wupT", kt)
                for ot in range(NK):
                    mm = nc.tensor.transpose(dst[:, ot * P:(ot + 1) * P],
                                             stage[SLOT["wup"]][:, ot, kt * P:(kt + 1) * P], ident[:])
                mm.then_inc(S["wupT_psum"], 1)
            for b in range(B):
                if b:
                    gate_and_lora_a(b - 1)
                    up(b - 1, 0)
                    z_to_tokens(b - 1)
                    up(b - 1, 1)
                p_transposes(b, (0, 1))
                if b:
                    up(b - 1, 2)
                    z_transposes(b - 1)
                p_transposes(b, (2, 3))
                if b:
                    lora_up(b - 1, 0)
                    lora_up(b - 1, 1)
                    lora_up(b - 1, 2)
                    if b + 1 < B:
                        up(b - 1, 3)
                        lora_up(b - 1, 3)
                pv(b)
                if b + 1 < B:
                    x1_transposes(b + 1)
                out_projection(b)
                if b + 1 < B:
                    qkv(b + 1, range(NK - 1))
                else:
                    up(b - 1, 3)
                    lora_up(b - 1, 3)
                x2_transposes(b)
                if b + 1 < B:
                    qkv(b + 1, range(NK - 1, NK))
                    scores(b + 1)
                    v_transposes(b + 1)
            b = B - 1
            gate_and_lora_a(b)
            up(b, 0)
            z_to_tokens(b)
            up(b, 1)
            up(b, 2)
            z_transposes(b)
            for t in range(NT):
                if t == NT - 1:
                    up(b, t)
                lora_up(b, t)

        @block.scalar
        def _(act):
            def h1_evacuate(b):
                for kt in range(NK):
                    act.wait_ge(S["x1T_psum"], NK * b + kt + 1)
                    if b == 0 and kt == 0:
                        act.wait_ge(S["modT_ready"], 2)
                    if b >= 2 and kt == 0:
                        act.wait_ge(S["h1_lo"], NK * b)
                    nc.scalar.activation(h1_full_at[b][:, kt, :], at("x1T", b, kt)[:], ACT.Identity,
                                         bias=modT["sa"][:, kt, b:b + 1], scale=modT["ca"][:, kt, b:b + 1]
                                         ).then_inc(S["h1_full"], 1)
                for kt in range(NK):
                    act.wait_ge(S["h1_full"], NK * b + kt + 1)
                    if b and kt == 0:
                        act.wait_ge(S["O_psum"], b)
                    nc.scalar.activation(ahi[:, kt, :], h1_full_at[b][:, kt, :], ACT.Copy).then_inc(S["h1_hi"], 1)

            def qkv_evacuate(b):
                for j in range(2):
                    act.wait_ge(S["qkv_psum"], 3 * b + j + 1)
                    if b:
                        act.wait_ge(S["S_psum"], NT * b)
                    if b == 0 and j == 0:
                        act.wait_ge(small_in, 16)
                    nc.scalar.activation(qk_hi[:, j, :], at("qkv", b, j)[:], ACT.Identity,
                                         bias=bqkv_col[:, j:j + 1]).then_inc(S["qk_hi_ready"], 1)
                act.wait_ge(S["qkv_psum"], 3 * b + 3)
                ins = nc.scalar.activation(vT[:], at("qkv", b, 2)[:], ACT.Identity, bias=bqkv_col[:, 2:3])
                ins.then_inc(S["vT_ready"], 1)

            def v_evacuate(b):
                act.wait_ge(S["V_psum"], b + 1)
                nc.scalar.activation(v_hi[:].rearrange("p t d -> p (t d)"), at("V", b)[:],
                                     ACT.Copy).then_inc(S["v_hi_ready"], 1)

            def softmax(b):
                for t in range(NT):
                    act.wait_ge(S["negmax_ready"], NT * b + t + 1)
                    if b and t == 0:
                        act.wait_ge(S["x2T_psum"], NK * b)
                    nc.scalar.activation(xn2_p[:, t, :], at("S", b, t)[:], ACT.Exp, bias=neg_max[:, t:t + 1],
                                         scale=SCORE_SCALE, accum_out=row_sum[:, t:t + 1]).then_inc(S["p_ready"], 1)

            def pt_hi(b, tiles):
                for t in tiles:
                    act.wait_ge(S["PT_psum"], NT * b + t + 1)
                    nc.scalar.activation(ahi[:, :, t * P:(t + 1) * P],
                                         at("PT", b, t)[:].rearrange("p (k q) -> p k q", k=NT),
                                         ACT.Copy).then_inc(S["pt_hi"], 1)

            def h2_evacuate(b):
                for kt in range(NK):
                    n = NK * b + kt
                    act.wait_ge(S["x2T_psum"], n + 1)
                    if b == 0 and kt == 0:
                        act.wait_ge(S["modT_ready"], 4)
                    if b and kt == 0:
                        act.wait_ge(S["h2_lo"], NK * b)
                    nc.scalar.activation(h2_full_at[b][:, kt, :], at("x2T", b, kt)[:], ACT.Identity,
                                         bias=modT["sb"][:, kt, b:b + 1], scale=modT["cb"][:, kt, b:b + 1]
                                         ).then_inc(S["h2_full"], 1)

            def wo_split(b):
                act.wait_ge(S["wo_ga_ready"], b + 1)
                if b:
                    act.wait_ge(S["Y_psum"], NT * b)
                nc.scalar.activation(wo_hi[:], wo_ga[:], ACT.Copy).then_inc(S["wo_hi_ready"], 1)

            def mod_row_evacuate(s):
                n = MODT.index(s)
                act.wait_ge(S["mod_psum"], MOD_ORDER.index(s) + 1)
                if n >= 2:
                    act.wait_ge(S["modT_psum"], n - 1)
                nc.scalar.activation(mod_row[:, n % 2, :], at("mod", s)[0:B, :], ACT.Copy).then_inc(S["mod_row_ready"], 1)

            def gz_evacuate(b):
                act.wait_ge(S["gz_psum"], b + 1)
                if b:
                    act.wait_ge(S["zl_psum"], b)
                nc.scalar.activation(gz[:], at("gz", b)[0:2 * GZ, :], ACT.Copy).then_inc(S["gz_ready"], 1)

            def zT_evacuate(b):
                act.wait_ge(S["zT_psum"], b + 1)
                if b:
                    act.wait_ge(S["F_psum"], NT * b)
                nc.scalar.activation(zT[:], at("zT", b)[:], ACT.Copy).then_inc(S["zT_ready"], 1)

            act.wait_ge(S["cT_psum"], 1)
            nc.scalar.activation(silu_tmp[:, 0, :], at("cT")[:, 0:NK * B], ACT.Exp, scale=-1.0).then_inc(S["silu_step"], 1)
            mod_row_evacuate("sa")
            mod_row_evacuate("ca")
            act.wait_ge(wqkv_in, 16)
            nc.scalar.activation(wqkv_hi[:], stage[SLOT["wqkv"]][:, :, 0:3 * D], ACT.Copy).then_inc(S["wqkv_hi_ready"], 1)
            h1_evacuate(0)
            qkv_evacuate(0)
            softmax(0)
            v_evacuate(0)
            act.wait_ge(S["gateA_psum"], 1)
            nc.scalar.activation(gzw[:, :, 0, :], at("gateA")[:, 0:NK * GZ].rearrange("p (k g) -> p k g", k=NK),
                                 ACT.Copy).then_inc(S["gzw_hi_ready"], 1)
            mod_row_evacuate("sb")
            mod_row_evacuate("cb")
            act.wait_ge(S["loraB_psum"], 1)
            nc.scalar.activation(lb_hi, at("loraB")[:], ACT.Copy).then_inc(S["lb_hi_ready"], 1)
            for kt in range(NK):
                act.wait_ge(S["wupT_psum"], kt + 1)
                nc.scalar.activation(wup_hi[:, kt, :], at("wupT", kt)[:], ACT.Copy).then_inc(S["wup_hi_ready"], 1)
            wo_split(0)
            for b in range(B):
                if b:
                    gz_evacuate(b - 1)
                    wo_split(b)
                pt_hi(b, (0, 1))
                if b:
                    zT_evacuate(b - 1)
                pt_hi(b, (2, 3))
                act.wait_ge(S["O_psum"], b + 1)
                nc.scalar.activation(o_hi[:], at("O", b)[:], ACT.Copy).then_inc(S["o_hi_ready"], 1)
                if b + 1 < B:
                    h1_evacuate(b + 1)
                h2_evacuate(b)
                if b + 1 < B:
                    qkv_evacuate(b + 1)
                    softmax(b + 1)
                    v_evacuate(b + 1)
            gz_evacuate(B - 1)
            zT_evacuate(B - 1)

        @block.vector
        def _(dve):
            def ln1_moments(b):
                for t in range(NT):
                    if b == 0:
                        dve.wait_ge(x0_in[t], 16)
                    elif t == 0:
                        dve.wait_ge(x_in[b], 16)
                        dve.wait_ge(S["xn1_ready"], NT * b)
                    nc.vector.bn_stats(stats[:, 0, t, :], xs[:, b, t, :]).then_inc(S["ln1_stats"], 1)
                for t in range(NT):
                    dve.wait_ge(S["ln1_stats"], NT * b + t + 1)
                    nc.vector.bn_aggr(moments[:, 0, t, :], stats[:, 0, t, :]).then_inc(S["ln1_aggr"], 1)
                dve.wait_ge(S["ln1_aggr"], NT * (b + 1))
                nc.vector.tensor_scalar(var_eps[:, 0, :], moments[:, 0, :, 1], LN_EPS, None,
                                        ALU.add).then_inc(S["ln1_var"], 1)

            def ln1_normalise(b):
                dve.wait_ge(S["ln1_rstd"], b + 1)
                if b:
                    dve.wait_ge(S["x1T_psum"], NK * b)
                for t in range(NT):
                    nc.vector.tensor_scalar(xn1[:, t, :], xs[:, b, t, :], moments[:, 0, t, 0:1], rstd[:, 0, t:t + 1],
                                            ALU.subtract, ALU.mult).then_inc(S["xn1_ready"], 1)

            def ln2_normalise(b, t):
                dve.wait_ge(S["ln2_rstd"], NT * b + t + 1)
                nc.vector.tensor_scalar(xn2_p[:, t, :], xs[:, b, t, :], moments[:, 1, t, 0:1], rstd[:, 1, t:t + 1],
                                        ALU.subtract, ALU.mult).then_inc(S["xn2_ready"], 1)

            def mod_evacuate(s):
                dve.wait_ge(S["modT_psum"], MODT.index(s) + 1)
                nc.vector.tensor_scalar(modT[s][:].rearrange("p k b -> p (k b)"), at("modT", s)[:, 0:NK * B],
                                        1.0 if s in ("ca", "cb") else 0.0, None,
                                        ALU.add).then_inc(S["modT_ready"], 1)

            def gate_rows(i, s):
                done = GATE_STEPS * i
                dve.wait_ge(S["mod_psum"], MOD_ORDER.index(s) + 1)
                nc.vector.tensor_copy(gate_tmp[:, 2, :], at("mod", s)[0:B, :]).then_inc(S["gate_step"], 1)
                dve.wait_ge(S["gate_step"], done + 1)
                nc.vector.scalar_tensor_tensor(gate_tmp[:, 0, :], gate_tmp[:, 2, :], -1.0, gate_tmp[:, 2, :], ALU.mult,
                                               ALU.max).then_inc(S["gate_step"], 1)
                nc.vector.tensor_scalar(gate_tmp[:, 1, :], gate_tmp[:, 2, :], 0.0, 2.0, ALU.is_ge,
                                        ALU.mult).then_inc(S["gate_step"], 1)
                dve.wait_ge(S["gate_step"], done + 3)
                nc.vector.tensor_scalar(gate_tmp[:, 2, :], gate_tmp[:, 0, :], GATE_FLOOR, None,
                                        ALU.max).then_inc(S["gate_step"], 1)
                dve.wait_ge(S["gate_step"], done + 4)
                nc.vector.scalar_tensor_tensor(gates[:, i, :], gate_tmp[:, 1, :], -1.0, gate_tmp[:, 2, :], ALU.add,
                                               ALU.mult).then_inc(S["gates_ready"], 1)
                dve.wait_ge(S["gates_ready"], i + 1)

            def h2_high(b):
                for kt in range(NK):
                    dve.wait_ge(S["h2_full"], NK * b + kt + 1)
                    if b and kt == 0:
                        dve.wait_ge(S["F_psum"], NT * b)
                    nc.vector.tensor_copy(h2hi[:, kt, :], h2_full_at[b][:, kt, :]).then_inc(S["h2_hi"], 1)
                    if b + 1 == B:
                        dve.wait_ge(S["h2_hi"], NK * b + kt + 1)
                        nc.vector.tensor_tensor(h2lo[:, kt, :], h2_full_at[b][:, kt, :], h2hi[:, kt, :].bitcast(F32),
                                                ALU.subtract).then_inc(S["h2_lo"], 1)

            def qk_low(b):
                for j in range(2):
                    dve.wait_ge(S["qk_hi_ready"], 2 * b + j + 1)
                    nc.vector.scalar_tensor_tensor(qk_lo[:, j, :], at("qkv", b, j)[:], bqkv_col[:, j:j + 1],
                                                   qk_hi[:, j, :].bitcast(F32), ALU.add,
                                                   ALU.subtract).then_inc(S["qk_lo_ready"], 1)

            def v_low(b):
                dve.wait_ge(S["v_hi_ready"], b + 1)
                nc.vector.tensor_tensor(v_lo[:].rearrange("p t d -> p (t d)"), at("V", b)[:],
                                        v_hi[:].bitcast(F32).rearrange("p t d -> p (t d)"),
                                        ALU.subtract).then_inc(S["v_lo_ready"], 1)

            def maxima(b):
                for t in range(NT):
                    dve.wait_ge(S["S_psum"], NT * b + t + 1)
                    nc.vector.reduce_max(row_max[:, t:t + 1], at("S", b, t)[:], AX_X).then_inc(S["max_ready"], 1)
                    dve.wait_ge(S["max_ready"], NT * b + t + 1)
                    nc.vector.tensor_scalar(neg_max[:, t:t + 1], row_max[:, t:t + 1], -SCORE_SCALE, None,
                                            ALU.mult).then_inc(S["negmax_ready"], 1)

            def pt_low(b, t):
                dve.wait_ge(S["pt_hi"], NT * b + t + 1)
                q = slice(t * P, (t + 1) * P)
                nc.vector.tensor_tensor(alo[:, :, q], at("PT", b, t)[:].rearrange("p (k q) -> p k q", k=NT),
                                        ahi[:, :, q].bitcast(F32), ALU.subtract).then_inc(S["pt_lo"], 1)

            def inverse_sums(b):
                dve.wait_ge(S["p_ready"], NT * (b + 1))
                nc.vector.reciprocal(row_inv[:], row_sum[:]).then_inc(S["inv_ready"], 1)

            def o_low(b):
                dve.wait_ge(S["o_hi_ready"], b + 1)
                nc.vector.tensor_tensor(o_lo[:], at("O", b)[:], o_hi[:].bitcast(F32),
                                        ALU.subtract).then_inc(S["o_lo_ready"], 1)

            def attention_residual(b):
                dve.wait_ge(S["inv_ready"], b + 1)
                for t in range(NT):
                    dve.wait_ge(S["Y_psum"], NT * b + t + 1)
                    dve.wait_ge(S["xb_ready"], NT * b + t + 1)
                    nc.vector.scalar_tensor_tensor(xs[:, b, t, :], at("Y", b, t)[:], row_inv[:, t:t + 1],
                                                   xs[:, b, t, :], ALU.mult, ALU.add).then_inc(S["x2_ready"], 1)

            def ln2(b):
                if b:
                    dve.wait_ge(S["xn2_ready"], NT * b)
                for t in range(NT + 2):
                    if t < NT:
                        dve.wait_ge(S["x2_ready"], NT * b + t + 1)
                        nc.vector.bn_stats(stats[:, 1, t, :], xs[:, b, t, :]).then_inc(S["ln2_stats"], 1)
                    if 1 <= t <= NT:
                        dve.wait_ge(S["ln2_stats"], NT * b + t)
                        nc.vector.bn_aggr(moments[:, 1, t - 1, :], stats[:, 1, t - 1, :]).then_inc(S["ln2_aggr"], 1)
                        dve.wait_ge(S["ln2_aggr"], NT * b + t)
                        nc.vector.tensor_scalar(var_eps[:, 1, t - 1:t], moments[:, 1, t - 1, 1:2], LN_EPS, None,
                                                ALU.add).then_inc(S["ln2_var"], 1)
                    if t >= 2:
                        ln2_normalise(b, t - 2)

            def choose_expert(b):
                parts = at("zl", b)[:, 0:NT * 2 * GZ].rearrange("p (t a g) -> p t a g", t=NT, a=2)
                done = Z_STEPS * b
                dve.wait_ge(S["zl_psum"], b + 1)
                if b == 0:
                    dve.wait_ge(eb_in, 16 * NT)
                nc.vector.tensor_tensor(zl_tmp[:], parts[:, :, 1, :], logit_bias[:], ALU.add).then_inc(S["z_step"], 1)
                dve.wait_ge(S["z_step"], done + 1)
                nc.vector.tensor_tensor(zl[:], parts[:, :, 0, :], zl_tmp[:], ALU.add).then_inc(S["z_step"], 1)
                dve.wait_ge(S["z_step"], done + 2)
                nc.vector.reduce_max(z_max[:, 0, :], zl[:, :, 0:E], AX_X).then_inc(S["z_step"], 1)
                dve.wait_ge(S["z_step"], done + 3)
                nc.vector.tensor_tensor(z_arg[:, 0], zl[:, :, 0:E], z_max[:, 0, :].unsqueeze(2).to_broadcast([P, NT, E]),
                                        ALU.is_equal).then_inc(S["z_step"], 1)
                dve.wait_ge(S["z_step"], done + 4)
                nc.vector.tensor_tensor(z_arg[:, 1], z_arg[:, 0], first_wins[:], ALU.mult).then_inc(S["z_step"], 1)
                dve.wait_ge(S["z_step"], done + 5)
                nc.vector.reduce_max(z_max[:, 1, :], z_arg[:, 1], AX_X).then_inc(S["z_step"], 1)
                dve.wait_ge(S["z_step"], done + 6)
                nc.vector.tensor_tensor(z_arg[:, 2], z_arg[:, 1], z_max[:, 1, :].unsqueeze(2).to_broadcast([P, NT, E]),
                                        ALU.is_equal).then_inc(S["z_step"], 1)
                dve.wait_ge(S["z_step"], done + 7)
                nc.vector.tensor_tensor(zm[:].rearrange("p t (e r) -> p t e r", e=E),
                                        zl[:, :, E:GZ].rearrange("p t (e r) -> p t e r", e=E),
                                        z_arg[:, 2].unsqueeze(3).to_broadcast([P, NT, E, R]),
                                        ALU.mult).then_inc(S["z_step"], 1)
                dve.wait_ge(S["z_step"], done + 8)
                if b:
                    dve.wait_ge(S["zT_psum"], b)
                twice = zm[:].unsqueeze(2).to_broadcast([P, NT, 2, ER])
                nc.vector.tensor_copy(zst[:, :, :, 0, :], twice).then_inc(S["zst_ready"], 1)
                dve.wait_ge(S["zst_ready"], 2 * b + 1)
                nc.vector.tensor_tensor(zst[:, :, :, 1, :], twice, zst[:, :, :, 0, :].bitcast(F32),
                                        ALU.subtract).then_inc(S["zst_ready"], 1)

            def gate_ffn(b, t):
                n = NT * b + t
                dve.wait_ge(S["F_psum"], n + 1)
                if t == 0:
                    dve.wait_ge(gb_bc_in[b % 2], 16 * (b // 2 + 1))
                if n >= 2:
                    dve.wait_ge(S["out_ready"], n - 1)
                nc.vector.tensor_tensor(f_gb[:, n % 2, :], at("F", b, t)[:], gb_bc[:, b % 2, :],
                                        ALU.mult).then_inc(S["f_gb_ready"], 1)

            nc.vector.memset(neg_half[:], -0.5).then_inc(S["dve_const"], 1)
            for e in range(E):
                nc.vector.memset(first_wins[:, :, e], float(E - e)).then_inc(S["dve_const"], 1)
            nc.vector.memset(logit_bias[:], 0.0).then_inc(S["dve_const"], 1)
            dve.wait_ge(S["silu_step"], 1)
            nc.vector.tensor_scalar(silu_tmp[:, 1, :], silu_tmp[:, 0, :], 1.0, None, ALU.add).then_inc(S["silu_step"], 1)
            dve.wait_ge(S["silu_step"], 2)
            nc.vector.reciprocal(silu_tmp[:, 2, :], silu_tmp[:, 1, :]).then_inc(S["silu_step"], 1)
            dve.wait_ge(S["silu_step"], 3)
            nc.vector.tensor_tensor(siluT[:], at("cT")[:, 0:NK * B], silu_tmp[:, 2, :], ALU.mult).then_inc(S["siluT_ready"], 1)
            ln1_moments(0)
            ln1_normalise(0)
            mod_evacuate("sa")
            mod_evacuate("ca")
            dve.wait_ge(S["wqkv_hi_ready"], 1)
            nc.vector.tensor_tensor(wqkv_lo[:], stage[SLOT["wqkv"]][:, :, 0:3 * D], wqkv_hi[:].bitcast(F32),
                                    ALU.subtract).then_inc(S["wqkv_lo_ready"], 1)
            dve.wait_ge(small_in, 16)
            qk_low(0)
            gate_rows(0, "ga")
            maxima(0)
            v_low(0)
            dve.wait_ge(S["gzw_hi_ready"], 1)
            nc.vector.tensor_tensor(gzw[:, :, 1, :], at("gateA")[:, 0:NK * GZ].rearrange("p (k g) -> p k g", k=NK),
                                    gzw[:, :, 0, :].bitcast(F32), ALU.subtract).then_inc(S["gzw_lo_ready"], 1)
            dve.wait_ge(lora_b_in, 16 * E)
            for a in range(4):
                nc.vector.tensor_copy(lora_b_rep[:, :, a, :], lora_b_raw[:]).then_inc(S["loraB_rep_ready"], 1)
            gate_rows(1, "gb")
            ln1_moments(1)
            mod_evacuate("sb")
            dve.wait_ge(S["lb_hi_ready"], 1)
            nc.vector.tensor_copy(lbw[0:2 * ER, :], lb_hi[0:2 * ER, :].bitcast(F32)).then_inc(S["lbw_ready"], 1)
            nc.vector.tensor_tensor(lbw[2 * ER:4 * ER, :], at("loraB")[2 * ER:4 * ER, :],
                                    lb_hi[2 * ER:4 * ER, :].bitcast(F32), ALU.subtract).then_inc(S["lbw_ready"], 1)
            mod_evacuate("cb")
            ln1_normalise(1)
            for kt in range(NK):
                dve.wait_ge(S["wup_hi_ready"], kt + 1)
                nc.vector.tensor_tensor(wup_lo[:, kt, :], at("wupT", kt)[:], wup_hi[:, kt, :].bitcast(F32),
                                        ALU.subtract).then_inc(S["wup_lo_ready"], 1)
            for b in range(B):
                if b:
                    if b + 1 < B:
                        ln1_moments(b + 1)
                    choose_expert(b - 1)
                for t in range(NT):
                    pt_low(b, t)
                    if b and b + 1 < B and t == 1:
                        ln1_normalise(b + 1)
                inverse_sums(b)
                if b:
                    gate_ffn(b - 1, 0)
                    gate_ffn(b - 1, 1)
                    gate_ffn(b - 1, 2)
                    if b + 1 < B:
                        gate_ffn(b - 1, 3)
                o_low(b)
                attention_residual(b)
                ln2(b)
                if b + 1 == B:
                    gate_ffn(b - 1, 3)
                h2_high(b)
                if b + 1 < B:
                    qk_low(b + 1)
                    maxima(b + 1)
                    v_low(b + 1)
            choose_expert(B - 1)
            for t in range(NT):
                gate_ffn(B - 1, t)

        @block.gpsimd
        def _(pool):
            def ln1_deviation(b):
                pool.wait_ge(S["ln1_var"], b + 1)
                if b == 0:
                    pool.wait_ge(S["dve_const"], 1)
                nc.gpsimd.tensor_tensor(rstd[:, 0, :], var_eps[:, 0, :], neg_half[:], ALU.pow).then_inc(S["ln1_rstd"], 1)

            def output_weights(b):
                pool.wait_ge(ga_bc_in[b % 2], 16 * (b // 2 + 1))
                if b == 0:
                    pool.wait_ge(wo_in, 16)
                    pool.wait_ge(bo_in, 16)
                else:
                    pool.wait_ge(S["wo_hi_ready"], b)
                    pool.wait_ge(S["wo_lo_ready"], b)
                nc.gpsimd.tensor_tensor(wo_ga[:], wo_raw[:], ga_bc[:, b % 2, :], ALU.mult).then_inc(S["wo_ga_ready"], 1)
                if b:
                    pool.wait_ge(S["xb_ready"], NT * b)
                nc.gpsimd.tensor_tensor(gabo[:], bo_bc[:], ga_bc[:, b % 2, :], ALU.mult).then_inc(S["gabo_ready"], 1)
                pool.wait_ge(S["wo_hi_ready"], b + 1)
                nc.gpsimd.tensor_tensor(wo_lo[:], wo_ga[:], wo_hi[:].bitcast(F32), ALU.subtract).then_inc(S["wo_lo_ready"], 1)
                pool.wait_ge(S["gabo_ready"], b + 1)
                pool.wait_ge(S["xn1_ready"], NT * (b + 1))
                for t in range(NT):
                    nc.gpsimd.tensor_tensor(xs[:, b, t, :], xs[:, b, t, :], gabo[:], ALU.add).then_inc(S["xb_ready"], 1)

            def ln2_deviation(b):
                for t in range(NT):
                    pool.wait_ge(S["ln2_var"], NT * b + t + 1)
                    nc.gpsimd.tensor_tensor(rstd[:, 1, t:t + 1], var_eps[:, 1, t:t + 1], neg_half[:, 0:1],
                                            ALU.pow).then_inc(S["ln2_rstd"], 1)

            def h1_low(b):
                for kt in range(NK):
                    n = NK * b + kt
                    pool.wait_ge(S["h1_hi"], n + 1)
                    nc.gpsimd.tensor_tensor(alo[:, kt, :], h1_full_at[b][:, kt, :], ahi[:, kt, :].bitcast(F32),
                                            ALU.subtract).then_inc(S["h1_lo"], 1)

            def h2_low(b):
                for kt in range(NK):
                    n = NK * b + kt
                    pool.wait_ge(S["h2_hi"], n + 1)
                    nc.gpsimd.tensor_tensor(h2lo[:, kt, :], h2_full_at[b][:, kt, :], h2hi[:, kt, :].bitcast(F32),
                                            ALU.subtract).then_inc(S["h2_lo"], 1)


            def outputs(b, tiles):
                for t in tiles:
                    n = NT * b + t
                    pool.wait_ge(S["f_gb_ready"], n + 1)
                    nc.gpsimd.tensor_tensor(xs[:, b, t, :], xs[:, b, t, :], f_gb[:, n % 2, :], ALU.add).then_inc(S["out_ready"], 1)

            nc.gpsimd.memset(ident[:], 0.0).then_inc(S["const_ready"], 1)
            pool.wait_ge(S["const_ready"], 1)
            nc.gpsimd.affine_select(out=ident[:], in_=ident[:], compare_op=ALU.not_equal, fill=1.0, base=0,
                                    pattern=[[-1, P]], channel_multiplier=1).then_inc(S["const_ready"], 1)
            ln1_deviation(0)
            h1_low(0)
            for b in range(B):
                if b + 1 < B:
                    ln1_deviation(b + 1)
                output_weights(b)
                if b:
                    outputs(b - 1, range(NT if b + 1 < B else NT - 1))
                if b + 1 < B:
                    h1_low(b + 1)
                ln2_deviation(b)
                if b + 1 < B:
                    h2_low(b)
                else:
                    outputs(b - 1, (NT - 1,))
            outputs(B - 1, range(NT))


_INS = ["L0_attn_x", "L0_attn_Wqkv", "L0_attn_bqkv", "L0_attn_Wo", "L0_attn_bo", "L0_ffn_W_up", "L0_ffn_gate_w",
        "L0_ffn_expert_bias", "L0_ffn_lora_A", "L0_ffn_lora_B", "L0_c", "L0_wmod"]


def kernel(**inputs):
    import numpy as _np
    import concourse.bacc as _bacc
    from concourse.bass_utils import run_bass_kernel_spmd as _run

    nc = _bacc.Bacc("TRN2", target_bir_lowering=False, num_devices=1)
    arrays, args = {}, []
    for name in _INS:
        a = _np.ascontiguousarray(inputs[name])
        arrays[f"in_{name}_dram"] = a
        args.append(nc.dram_tensor(f"in_{name}_dram", a.shape, mybir.dt.from_np(a.dtype), kind="ExternalInput").ap())
    out = nc.dram_tensor("out_0_dram", (B, T, H), F32, kind="ExternalOutput").ap()
    adaln_block(nc, *args, out)
    r = _run(nc, [arrays], core_ids=[0])
    return r.results[0]["out_0_dram"]
```

```python
from contextlib import ExitStack

import concourse.bass as bass
from concourse import mybir

ALU = mybir.AluOpType
ACT = mybir.ActivationFunctionType
AX_X = mybir.AxisListType.X
F32 = mybir.dt.float32
F32R = mybir.dt.float32r

P = 128
B = 4
T = 512
H = 512
D = 128
E = 4
R = 8
NT = T // P
NK = H // P
ER = E * R
GZ = E + ER
LN_EPS = 1e-5
SCORE_SCALE = float(D) ** -0.5
GATE_FLOOR = 0.25
MOD_ORDER = ("sa", "ca", "ga", "sb", "cb", "gb")
MODT = ("sa", "ca", "sb", "cb")
GATE_STEPS = 3
Z_STEPS = 8


def psum_plan():
    order = [("tp", "cT"), ("mm", "mod", "sa"), ("mm", "mod", "ca"), ("ff", "modT", "sa"), ("ff", "modT", "ca")]

    def scores(b):
        return [("mm", "S", b, t) for t in range(NT - 1)] + [("tp", "S", b, NT - 1), ("tp", "V", b)]

    def turned(kind, b, kts):
        return [("ff" if kt in (0, 3) and kind == "x2T" else "tp", kind, b, kt) for kt in kts]

    order += [("tp" if kt < 2 else "ff", "x1T", 0, kt) for kt in range(NK)] + [("mm", "qkv", 0, j) for j in range(3)]
    order += [("ff", "mod", "ga")] + scores(0) + [("ff", "gateA"), ("ff", "loraB")]
    for b in range(B):
        if b:
            order += [("ff", "gz", b - 1), ("ff", "F", b - 1, 0), ("ff", "F", b - 1, 1)]
        else:
            order += [("ff", "mod", "sb")]
        last = b + 1 == B
        order += [("tp", "PT", b, 0), ("tp", "PT", b, 1), ("mm", "PT", b, 2), ("mm", "PT", b, 3)]
        if b:
            order += [("tp", "zl", b - 1), ("ff", "F", b - 1, 2)]
        if not last:
            order += turned("x1T", b + 1, (0,))
        order += [("mm", "O", b)]
        if not last:
            order += turned("x1T", b + 1, (1,))
        if b:
            order += [("tp", "zT", b - 1)] + [("mm", "Y", b, t) for t in range(NT)]
            if not last:
                order += turned("x1T", b + 1, (2, 3)) + [("mm", "qkv", b + 1, j) for j in range(3)]
            else:
                order += [("ff", "F", b - 1, 3)]
        else:
            order += turned("x1T", b + 1, (2, 3))
            order += [("mm", "qkv", b + 1, j) for j in range(3)]
            order += [("tp" if t < 2 else "ff", "Y", b, t) for t in range(NT)]
            order += [("ff", "wupT", 0), ("ff", "wupT", 1), ("ff", "mod", "cb"), ("ff", "modT", "sb"), ("ff", "modT", "cb"),
                      ("ff", "mod", "gb")]
        if not last:
            order += turned("x2T", b, range(NK))
            if b:
                order += [("ff", "F", b - 1, 3)]
        if b == 0:
            order += [("ff", "wupT", 2), ("ff", "wupT", 3)]
        if b + 1 < B:
            order += scores(b + 1)
    b = B - 1
    order += [("tp" if t < 2 else "mm", "x2T", b, t) for t in range(NT)]
    order += [("ff", "gz", b), ("ff", "F", b, 0), ("ff", "F", b, 1), ("tp", "zl", b), ("mm", "F", b, 2),
              ("mm", "F", b, 3), ("tp", "zT", b)]
    banks = {"mm": (0, 1, 2), "tp": (3, 4), "ff": (5, 6, 7)}
    place, earlier, taken, holds = {}, {}, dict.fromkeys(banks, 0), [None] * 8
    for ring, *name in order:
        bank = banks[ring][taken[ring] % len(banks[ring])]
        taken[ring] += 1
        place[tuple(name)] = bank
        earlier[tuple(name)] = holds[bank]
        holds[bank] = tuple(name)
    return place, earlier


def adaln_block(nc: bass.Bass, x, wqkv, bqkv, wo, bo, wup, gate_w, expert_bias, lora_a, lora_b, c, wmod, out):
    place, earlier = psum_plan()
    with ExitStack() as ctx:
        def sb(name, shape, dt=F32):
            return ctx.enter_context(nc.sbuf_tensor(name, shape, dt))

        def sem(name):
            return ctx.enter_context(nc.semaphore(name))

        bank = [ctx.enter_context(nc.psum_tensor(f"bank{i}", [P, 512], F32)) for i in range(8)]

        ident = sb("ident", [P, P])
        neg_half = sb("neg_half", [P, NT])
        first_wins = sb("first_wins", [P, NT, E])
        logit_bias = sb("logit_bias", [P, NT, GZ])
        c_row = sb("c_row", [B, H])
        silu_split = sb("silu_split", [P, NK, 2, B], F32R)
        modT = {s: sb(f"modT_{s}", [P, NK, B]) for s in MODT}
        gate_tmp = sb("gate_tmp", [B, 3, H])
        silu_tmp = sb("silu_tmp", [P, 3, NK * B])
        mod_sum = sb("mod_sum", [P, NK * B])
        mod_row = sb("mod_row", [2 * B, 2, H])
        gates = sb("gates", [B, 2, H])
        ga_bc = sb("ga_bc", [P, 2, H])
        gb_bc = sb("gb_bc", [P, 2, H])
        bo_bc = sb("bo_bc", [P, H])
        gabo = sb("gabo", [P, H])
        bqkv_col = sb("bqkv_col", [P, 3])
        ga_rows = sb("ga_rows", [GZ, H])
        lora_b_raw = sb("lora_b_raw", [P, NK, ER])
        stage = [sb(f"stage{i}", [P, NK, H]) for i in range(3)]
        wqkv_hi = sb("wqkv_hi", [P, NK, 3 * D], F32R)
        wqkv_lo = sb("wqkv_lo", [P, NK, 3 * D], F32R)
        wup_hi = sb("wup_hi", [P, NK, H], F32R)
        wup_lo = sb("wup_lo", [P, NK, H], F32R)
        wo_raw = sb("wo_raw", [P, H])
        wo_ga = sb("wo_ga", [P, H])
        wo_hi = sb("wo_hi", [P, H], F32R)
        wo_lo = sb("wo_lo", [P, H], F32R)
        gzw = sb("gzw", [P, NK, 2, GZ], F32R)
        lbw = sb("lbw", [P, H], F32R)
        xs = sb("xs", [P, B, NT, H])
        xn1 = sb("xn1", [P, NT, H])
        xn2_p = sb("xn2_p", [P, NT, H])
        h1_full_at = [xn2_p] + [stage[0]] * (B - 1)
        h2_full_at = [stage[2]] * B
        ahi = sb("ahi", [P, NK, T], F32R)
        alo = sb("alo", [P, NK, T], F32R)
        h2hi = sb("h2hi", [P, NK, T], F32R)
        h2lo = sb("h2lo", [P, NK, T], F32R)
        mod_split = {s: (ahi, alo) if s == "ca" else (h2hi, h2lo) for s in MOD_ORDER}
        qk_hi = sb("qk_hi", [P, 2, T], F32R)
        qk_lo = sb("qk_lo", [P, 2, T], F32R)
        vT = sb("vT", [P, T])
        v_hi = sb("v_hi", [P, NT, D], F32R)
        v_lo = sb("v_lo", [P, NT, D], F32R)
        o_hi = sb("o_hi", [P, T], F32R)
        o_lo = sb("o_lo", [P, T], F32R)
        gz = sb("gz", [2 * GZ, T])
        zl_tmp = sb("zl_tmp", [P, NT, GZ])
        zl = sb("zl", [P, NT, GZ])
        z_arg = sb("z_arg", [P, 3, NT, E])
        z_max = sb("z_max", [P, 2, NT])
        zm = sb("zm", [P, NT, ER])
        zst = sb("zst", [P, NT, 2, 2, ER], F32R)
        zT = sb("zT", [P, T], F32R)
        f_gb = sb("f_gb", [P, 2, H])
        lora_b_rep = f_gb[:, 0, :].rearrange("p (k a z) -> p k a z", k=NK, a=4)
        lb_hi = wup_hi[:, NK - 1, :]
        stats = sb("stats", [P, 2, NT, 6])
        moments = sb("moments", [P, 2, NT, 2])
        var_eps = sb("var_eps", [P, 2, NT])
        rstd = sb("rstd", [P, 2, NT])
        shift = sb("shift", [P, NT])
        row_max = sb("row_max", [P, NT])
        neg_max = sb("neg_max", [P, NT])
        row_sum = sb("row_sum", [P, NT])
        row_inv = sb("row_inv", [P, NT])

        c_in, small_in, wo_in, ga_rows_in, lora_b_in = map(
            sem, ("c_in", "small_in", "wo_in", "ga_rows_in", "lora_b_in"))
        bo_in, eb_in = sem("bo_in"), sem("eb_in")
        wup_in = sem("wup_in")
        mod_in = {s: sem(f"mod_in_{s}") for s in ("ga", "gb", "sb", "cb")}
        first_mod_in = {s: [sem(f"first_mod_in_{s}{kt}") for kt in range(NK)] for s in ("sa", "ca")}
        wqkv_in = [sem(f"wqkv_in{kt}") for kt in range(NK)]
        x0_in = [sem(f"x0_in{t}") for t in range(NT)]
        x_in = [sem(f"x_in{b}") for b in range(B)]
        ga_bc_in = [sem(f"ga_bc_in{i}") for i in range(2)]
        gb_bc_in = [sem(f"gb_bc_in{i}") for i in range(2)]
        gates_out = sem("gates_out")
        stored = sem("stored")
        last_out_ready = sem("last_out_ready")
        names = """
            mod_hi mod_lo_dve mod_lo_pool mod_kt mod_sum_ready ln2_shift const_ready dve_const
            silu_step cT_psum mod_row_ready modT_psum modT_ready gate_step gates_ready wqkv_hi_ready
            wqkv_lo_ready wup_hi_ready wup_lo_ready wo_ga_ready wo_hi_ready wo_lo_ready gabo_ready
            wupT_psum gateA_psum gzw_hi_ready gzw_lo_ready loraB_rep_ready loraB_psum lb_hi_ready
            lbw_ready ln1_stats ln1_aggr ln1_var ln1_rstd xn1_ready x1T_psum h1_full h1_hi h1_lo
            qkv_psum qk_hi_ready qk_lo_ready vT_ready V_psum v_hi_ready v_lo_ready S_psum max_ready
            negmax_ready p_ready PT_psum pt_hi pt_lo O_psum o_hi_ready o_lo_ready inv_ready Y_psum
            xb_ready x2_ready ln2_stats ln2_aggr ln2_var ln2_rstd xn2_ready x2T_psum h2_full h2_hi
            h2_lo gz_psum gz_ready zl_psum z_step zst_ready zT_psum zT_ready F_psum f_gb_ready
            out_ready""".split()
        S = {n: sem(n) for n in names}

        def at(*name):
            return bank[place[name]]

        def last_read(kind, *of):
            b, i = (*of, 0, 0)[:2] if kind not in ("mod", "modT") else (0, 0)
            return {
                "cT": ("silu_step", 4), "gateA": ("gzw_lo_ready", 1), "loraB": ("lbw_ready", 2),
                "wupT": ("wup_lo_ready", b + 1),
                "x1T": ("h1_full", NK * b + i + 1), "x2T": ("h2_full", NK * b + (i + 1 if b + 1 < B else NK * (i + 1))),
                "qkv": ("vT_ready", b + 1) if i == 2 else ("qk_lo_ready", 2 * b + i + 1),
                "V": ("v_lo_ready", b + 1), "S": ("p_ready", NT * b + i + 1), "PT": ("pt_lo", NT * b + i + 1),
                "O": ("o_lo_ready", b + 1), "Y": ("x2_ready", NT * b + i + 1),
                "gz": ("gz_ready", b + 1), "zl": ("z_step", Z_STEPS * b + 2), "zT": ("zT_ready", b + 1),
                "F": ("f_gb_ready", NT * b + i + 1),
                "mod": ("mod_row_ready", MOD_ORDER.index(of[0]) + 1 if kind == "mod" else 0),
                "modT": ("mod_sum_ready", MODT.index(of[0]) + 1 if kind == "modT" else 0),
            }[kind]

        def gated(n):
            return f_gb[:, n % 2, :] if n < NT * (B - 1) else xn1[:, n % NT, :]

        gates_dram = nc.dram_tensor("gates_dram", (2, B, H), F32).ap()
        BY_POOL = {"sa": (0, 2), "ca": (0,), "ga": (0, 2), "sb": (0, 1), "cb": (0, 2), "gb": (0, 2)}

        def lo_by_pool(n, kt):
            return sum(len([k for k in BY_POOL[s] if i < n or k < kt]) for i, s in enumerate(MOD_ORDER[:n + 1]))

        def lo_by_dve(n, kt):
            return NK * n + kt - lo_by_pool(n, kt)

        wmod_v = wmod.rearrange("(k p) (s n) -> s p k n", p=P, n=H)
        SECTION = {"sa": 0, "ca": 1, "ga": 2, "sb": 3, "cb": 4, "gb": 5}
        x_v = x.rearrange("b (t p) h -> b p t h", p=P)
        out_v = out.rearrange("b (t p) h -> b p t h", p=P)
        raw = {"wqkv": stage[0], "sa": stage[1], "ca": stage[2], "ga": xs[:, 3], "sb": xs[:, 2],
               "cb": stage[1], "gb": stage[2], "wup": xs[:, 3]}

        block = ctx.enter_context(nc.Block())

        @block.sync
        def _(sp):
            sp.dma_start(c_row[:], c).then_inc(c_in, 16)

            def load_first(s):
                for kt in range(NK):
                    sp.dma_start(raw[s][:, kt, :], wmod_v[SECTION[s]][:, kt, :]).then_inc(first_mod_in[s][kt], 16)

            def slot_split(s):
                n = MOD_ORDER.index(s) + 1
                sp.wait_ge(S["mod_hi"], NK * n)
                sp.wait_ge(S["mod_lo_dve"], lo_by_dve(n, 0))
                if lo_by_pool(n, 0):
                    sp.wait_ge(S["mod_lo_pool"], lo_by_pool(n, 0))

            load_first("sa")
            load_first("ca")
            for t in range(NT):
                sp.dma_start(xs[:, 0, t, :], x_v[0, :, t, :]).then_inc(x0_in[t], 16)
            for kt in range(NK):
                sp.dma_start(raw["wqkv"][:, kt, 0:3 * D], wqkv[kt * P:(kt + 1) * P, :]).then_inc(wqkv_in[kt], 16)
            sp.dma_start(bqkv_col[:], bqkv.rearrange("(j d) -> d j", d=D),
                         allow_slow_non_contiguous=True).then_inc(small_in, 16)
            sp.dma_start(xs[:, 1], x_v[1]).then_inc(x_in[1], 16)
            sp.dma_start(xs[:, 3], wmod_v[SECTION["ga"]]).then_inc(mod_in["ga"], 16)
            sp.dma_start(ga_rows[0:E, :], gate_w).then_inc(ga_rows_in, 16)
            sp.dma_start(ga_rows[E:GZ, :], lora_a.rearrange("e r h -> (e r) h")).then_inc(ga_rows_in, 16)
            for e in range(E):
                sp.dma_start(lora_b_raw[:, :, e * R:(e + 1) * R],
                             lora_b[e].rearrange("(k p) r -> p k r", p=P)).then_inc(lora_b_in, 16)
            sp.dma_start(xs[:, 2], wmod_v[SECTION["sb"]]).then_inc(mod_in["sb"], 16)
            sp.dma_start(wo_raw[:], wo).then_inc(wo_in, 16)
            sp.dma_start(bo_bc[:], bo.partition_broadcast(P)).then_inc(bo_in, 16)
            sp.wait_ge(S["dve_const"], 2 + E)
            for t in range(NT):
                sp.dma_start(logit_bias[:, t, 0:E], expert_bias.partition_broadcast(P)).then_inc(eb_in, 16)

            def write_gate(i):
                sp.wait_ge(S["gates_ready"], i + 1)
                sp.dma_start(gates_dram[i], gates[:, i, :]).then_inc(gates_out, 16)
                sp.wait_ge(gates_out, 16 * (i + 1))

            def spread_gate(i, b):
                if b >= 2 and i == 0:
                    sp.wait_ge(S["wo_ga_ready"], b - 1)
                    sp.wait_ge(S["gabo_ready"], b - 1)
                if b >= 2 and i == 1:
                    sp.wait_ge(S["f_gb_ready"], NT * (b - 1))
                to, ready = ((ga_bc, ga_bc_in), (gb_bc, gb_bc_in))[i]
                sp.dma_start(to[:, b % 2, :], gates_dram[i, b].partition_broadcast(P)).then_inc(ready[b % 2], 16)

            slot_split("sa")
            sp.dma_start(raw["cb"][:], wmod_v[SECTION["cb"]]).then_inc(mod_in["cb"], 16)
            slot_split("ca")
            sp.dma_start(raw["gb"][:], wmod_v[SECTION["gb"]]).then_inc(mod_in["gb"], 16)
            slot_split("ga")
            sp.dma_start(raw["wup"], wup.rearrange("(o p) h -> p o h", p=P)).then_inc(wup_in, 16)
            write_gate(0)
            spread_gate(0, 0)
            spread_gate(0, 1)
            slot_split("sb")
            sp.dma_start(xs[:, 2], x_v[2]).then_inc(x_in[2], 16)
            sp.wait_ge(S["wupT_psum"], NK)
            sp.dma_start(xs[:, 3], x_v[3]).then_inc(x_in[3], 16)
            write_gate(1)
            spread_gate(1, 0)
            spread_gate(1, 1)
            for b in range(B):
                if b >= 1 and b + 1 < B:
                    spread_gate(0, b + 1)
                    spread_gate(1, b + 1)
                for t in range(NT) if b + 1 < B else (0, 2, 1, 3):
                    if b + 1 == B and t >= 2:
                        sp.wait_ge(last_out_ready, t - 1)
                    else:
                        sp.wait_ge(S["out_ready"], NT * b + t + 1)
                    sp.dma_start(out_v[b, :, t, :], xs[:, b, t, :]).then_inc(stored, 16)
            sp.wait_ge(stored, 16 * B * NT)

        @block.tensor
        def _(pe):
            def keep_warm(dst, n):
                for _ in range(n):
                    nc.tensor.matmul(dst[:, 0:P], ident[:], ident[:], start=True, stop=True)

            def open_bank(*name):
                before = earlier[name]
                if before is not None:
                    ready, count = last_read(*before)
                    pe.wait_ge(S[ready], count)
                return at(*name)

            def products(dst, pairs, first=True, last=True):
                total = 3 * len(pairs)
                i = 0
                for (w_hi, w_lo), (m_hi, m_lo) in pairs:
                    for w, m in ((w_hi, m_lo), (w_lo, m_hi), (w_hi, m_hi)):
                        mm = nc.tensor.matmul(dst, w, m, start=first and i == 0, stop=last and i == total - 1)
                        i += 1
                return mm

            def mod_rows(s, kts=range(NK)):
                n = MOD_ORDER.index(s)
                dst = open_bank("mod", s) if kts[0] == 0 else at("mod", s)
                for kt in kts:
                    pe.wait_ge(S["mod_hi"], NK * n + kt + 1)
                    pe.wait_ge(S["mod_lo_dve"], lo_by_dve(n, kt + 1))
                    if lo_by_pool(n, kt + 1):
                        pe.wait_ge(S["mod_lo_pool"], lo_by_pool(n, kt + 1))
                    w_hi, w_lo = (part[:, kt, :] for part in mod_split[s])
                    if s in MODT:
                        both = silu_split[:, kt].rearrange("p a b -> p (a b)")
                        nc.tensor.matmul(dst[0:2 * B, :], both, w_lo, start=kt == 0, stop=False)
                        mm = nc.tensor.matmul(dst[0:2 * B, :], both, w_hi, start=False, stop=kt == NK - 1)
                    else:
                        mm = products(dst[0:B, :], [((silu_split[:, kt, 0, :], silu_split[:, kt, 1, :]), (w_hi, w_lo))],
                                      first=kt == 0, last=kt == NK - 1)
                    mm.then_inc(S["mod_kt"], 1)

            def mod_columns(s):
                n = MODT.index(s)
                dst = open_bank("modT", s)
                pe.wait_ge(S["mod_row_ready"], MOD_ORDER.index(s) + 1)
                for kt in range(NK):
                    mm = nc.tensor.transpose(dst[:, kt * 2 * B:(kt + 1) * 2 * B], mod_row[:, n % 2, kt * P:(kt + 1) * P],
                                             ident[0:2 * B, 0:2 * B])
                mm.then_inc(S["modT_psum"], 1)

            def x1_transposes(b, kts):
                pe.wait_ge(S["xn1_ready"], NT * (b + 1))
                for kt in kts:
                    dst = open_bank("x1T", b, kt)
                    for t in range(NT):
                        mm = nc.tensor.transpose(dst[:, t * P:(t + 1) * P], xn1[:, t, kt * P:(kt + 1) * P], ident[:])
                    mm.then_inc(S["x1T_psum"], 1)

            def qkv(b, kts):
                for kt in kts:
                    if b == 0:
                        pe.wait_ge(S["wqkv_hi_ready"], kt + 1)
                        pe.wait_ge(S["wqkv_lo_ready"], kt + 1)
                    pe.wait_ge(S["h1_hi"], NK * b + kt + 1)
                    pe.wait_ge(S["h1_lo"], NK * b + kt + 1)
                    for j in range(3):
                        f = slice(j * D, (j + 1) * D)
                        dst = open_bank("qkv", b, j) if kt == 0 else at("qkv", b, j)
                        mm = products(dst[:], [((wqkv_hi[:, kt, f], wqkv_lo[:, kt, f]), (ahi[:, kt, :], alo[:, kt, :]))],
                                      first=kt == 0, last=kt == NK - 1)
                        if kt == NK - 1:
                            mm.then_inc(S["qkv_psum"], 1)

            def v_transposes(b):
                dst = open_bank("V", b)
                pe.wait_ge(S["vT_ready"], b + 1)
                for t in range(NT):
                    mm = nc.tensor.transpose(dst[:, t * D:(t + 1) * D], vT[:, t * P:(t + 1) * P], ident[:])
                mm.then_inc(S["V_psum"], 1)

            def scores(b):
                pe.wait_ge(S["qk_hi_ready"], 2 * (b + 1))
                pe.wait_ge(S["qk_lo_ready"], 2 * (b + 1))
                for t in range(NT):
                    dst = open_bank("S", b, t)
                    q = slice(t * P, (t + 1) * P)
                    products(dst[:], [((qk_hi[:, 0, q], qk_lo[:, 0, q]), (qk_hi[:, 1, :], qk_lo[:, 1, :]))]
                             ).then_inc(S["S_psum"], 1)

            def p_transposes(b, tiles):
                for t in tiles:
                    dst = open_bank("PT", b, t)
                    pe.wait_ge(S["p_ready"], NT * b + t + 1)
                    for kt in range(NT):
                        mm = nc.tensor.transpose(dst[:, kt * P:(kt + 1) * P], xn2_p[:, t, kt * P:(kt + 1) * P], ident[:])
                    mm.then_inc(S["PT_psum"], 1)

            def pv(b):
                dst = open_bank("O", b)
                pe.wait_ge(S["v_hi_ready"], b + 1)
                pe.wait_ge(S["v_lo_ready"], b + 1)
                pe.wait_ge(S["pt_hi"], NT * (b + 1))
                pe.wait_ge(S["pt_lo"], NT * (b + 1))
                products(dst[:], [((v_hi[:, kt, :], v_lo[:, kt, :]), (ahi[:, kt, :], alo[:, kt, :])) for kt in range(NT)]
                         ).then_inc(S["O_psum"], 1)

            def out_projection(b):
                pe.wait_ge(S["wo_hi_ready"], b + 1)
                pe.wait_ge(S["wo_lo_ready"], b + 1)
                pe.wait_ge(S["o_hi_ready"], b + 1)
                pe.wait_ge(S["o_lo_ready"], b + 1)
                for t in range(NT):
                    dst = open_bank("Y", b, t)
                    q = slice(t * P, (t + 1) * P)
                    products(dst[:], [((o_hi[:, q], o_lo[:, q]), (wo_hi[:], wo_lo[:]))]).then_inc(S["Y_psum"], 1)

            def x2_transposes(b, kts):
                pe.wait_ge(S["xn2_ready"], NT * (b + 1))
                for kt in kts:
                    dst = open_bank("x2T", b, kt)
                    for t in range(NT):
                        mm = nc.tensor.transpose(dst[:, t * P:(t + 1) * P], xn2_p[:, t, kt * P:(kt + 1) * P], ident[:])
                    mm.then_inc(S["x2T_psum"], 1)

            def start_ffn(b, kt):
                if kt == 0:
                    for name in (("gz", b), ("F", b, 0), ("F", b, 1)):
                        open_bank(*name)
                    if b == 0:
                        pe.wait_ge(S["gzw_hi_ready"], 1)
                        pe.wait_ge(S["gzw_lo_ready"], 1)
                        pe.wait_ge(S["wup_hi_ready"], NK)
                        pe.wait_ge(S["wup_lo_ready"], NK)
                w = gzw[:, kt, :, :].rearrange("p a g -> p (a g)")
                pe.wait_ge(S["h2_hi"], NK * b + kt + 1)
                nc.tensor.matmul(at("gz", b)[0:2 * GZ, :], w, h2hi[:, kt, :], start=kt == 0, stop=False)
                for t in (0, 1):
                    q = slice(t * P, (t + 1) * P)
                    nc.tensor.matmul(at("F", b, t)[:], h2hi[:, kt, q], wup_lo[:, kt, :], start=kt == 0, stop=False)
                    nc.tensor.matmul(at("F", b, t)[:], h2hi[:, kt, q], wup_hi[:, kt, :], start=False, stop=False)
                pe.wait_ge(S["h2_lo"], NK * b + kt + 1)
                mm = nc.tensor.matmul(at("gz", b)[0:2 * GZ, :], w, h2lo[:, kt, :], start=False, stop=kt == NK - 1)
                if kt == NK - 1:
                    mm.then_inc(S["gz_psum"], 1)
                for t in (0, 1):
                    q = slice(t * P, (t + 1) * P)
                    nc.tensor.matmul(at("F", b, t)[:], h2lo[:, kt, q], wup_hi[:, kt, :], start=False, stop=False)

            def up(b, t, kts=range(NK)):
                dst = open_bank("F", b, t) if kts[0] == 0 else at("F", b, t)
                q = slice(t * P, (t + 1) * P)
                products(dst[:], [((h2hi[:, kt, q], h2lo[:, kt, q]), (wup_hi[:, kt, :], wup_lo[:, kt, :]))
                                  for kt in kts], first=kts[0] == 0, last=False)

            def x2_transposes_of_tile(t):
                b = B - 1
                dst = open_bank("x2T", b, t)
                pe.wait_ge(S["xn2_ready"], NT * b + t + 1)
                for kt in range(NK):
                    mm = nc.tensor.transpose(dst[:, kt * P:(kt + 1) * P], xn2_p[:, t, kt * P:(kt + 1) * P], ident[:])
                mm.then_inc(S["x2T_psum"], 1)

            def gate_and_lora_a_of_tile(t):
                b = B - 1
                dst = open_bank("gz", b) if t == 0 else at("gz", b)
                pe.wait_ge(S["h2_hi"], NK * b + t + 1)
                pe.wait_ge(S["h2_lo"], NK * b + t + 1)
                q = slice(t * P, (t + 1) * P)
                for kt in range(NK):
                    w = gzw[:, kt, :, :].rearrange("p a g -> p (a g)")
                    nc.tensor.matmul(dst[0:2 * GZ, q], w, h2lo[:, kt, q], start=kt == 0, stop=False)
                    mm = nc.tensor.matmul(dst[0:2 * GZ, q], w, h2hi[:, kt, q], start=False, stop=kt == NK - 1)
                if t == NT - 1:
                    mm.then_inc(S["gz_psum"], 1)

            def z_to_tokens(b):
                dst = open_bank("zl", b)
                pe.wait_ge(S["gz_ready"], b + 1)
                for t in range(NT):
                    mm = nc.tensor.transpose(dst[:, t * 2 * GZ:(t + 1) * 2 * GZ], gz[:, t * P:(t + 1) * P],
                                             ident[0:2 * GZ, 0:2 * GZ])
                mm.then_inc(S["zl_psum"], 1)

            def z_transposes(b):
                dst = open_bank("zT", b)
                pe.wait_ge(S["zst_ready"], 2 * (b + 1))
                for t in range(NT):
                    mm = nc.tensor.transpose(dst[:, t * P:(t + 1) * P],
                                             zst[:, t].bitcast(F32).rearrange("p a s z -> p (a s z)"), ident[:])
                mm.then_inc(S["zT_psum"], 1)

            def lora_up(b, t):
                if b == 0 and t == 0:
                    pe.wait_ge(S["lbw_ready"], 2)
                if t == 0:
                    pe.wait_ge(S["zT_ready"], b + 1)
                nc.tensor.matmul(at("F", b, t)[:], zT[:, t * P:(t + 1) * P], lbw[:], start=False,
                                 stop=True).then_inc(S["F_psum"], 1)

            def gate_transposes():
                dst = open_bank("gateA")
                pe.wait_ge(ga_rows_in, 32)
                for kt in range(NK):
                    mm = nc.tensor.transpose(dst[:, kt * GZ:(kt + 1) * GZ], ga_rows[:, kt * P:(kt + 1) * P],
                                             ident[0:GZ, 0:GZ])
                mm.then_inc(S["gateA_psum"], 1)

            def lora_b_transposes():
                dst = open_bank("loraB")
                pe.wait_ge(S["loraB_rep_ready"], 4)
                for kt in range(NK):
                    mm = nc.tensor.transpose(dst[:, kt * P:(kt + 1) * P],
                                             lora_b_rep[:, kt].rearrange("p a z -> p (a z)"), ident[:])
                mm.then_inc(S["loraB_psum"], 1)

            def w_up_transposes(kts):
                pe.wait_ge(wup_in, 16)
                for kt in kts:
                    dst = open_bank("wupT", kt)
                    for ot in range(NK):
                        mm = nc.tensor.transpose(dst[:, ot * P:(ot + 1) * P],
                                                 raw["wup"][:, ot, kt * P:(kt + 1) * P], ident[:])
                    mm.then_inc(S["wupT_psum"], 1)

            pe.wait_ge(S["const_ready"], 2)
            keep_warm(bank[7], 8)
            dst = open_bank("cT")
            pe.wait_ge(c_in, 16)
            for kt in range(NK):
                mm = nc.tensor.transpose(dst[:, B * kt:B * kt + B], c_row[:, kt * P:(kt + 1) * P], ident[0:B, 0:B])
            mm.then_inc(S["cT_psum"], 1)
            keep_warm(bank[7], 5)
            pe.wait_ge(S["silu_step"], 6)
            mod_rows("sa")
            mod_rows("ca")
            mod_columns("sa")
            mod_columns("ca")
            keep_warm(bank[7], 7)
            x1_transposes(0, range(NK))
            keep_warm(open_bank("qkv", 0, 0), 4)
            qkv(0, range(NK))
            mod_rows("ga")
            scores(0)
            v_transposes(0)
            gate_transposes()
            lora_b_transposes()
            mod_rows("sb", (0, 1))
            for b in range(B):
                if b:
                    for kt in range(NK):
                        start_ffn(b - 1, kt)
                last = b + 1 == B
                p_transposes(b, (0,))
                if b == 0:
                    keep_warm(open_bank("O", 0), 4)
                p_transposes(b, (1,))
                if b:
                    up(b - 1, 2, (0,))
                p_transposes(b, (2, 3))
                if b:
                    z_to_tokens(b - 1)
                    up(b - 1, 2, (1, 2))
                else:
                    keep_warm(at("O", 0), 4)
                if not last:
                    x1_transposes(b + 1, (0,))
                pv(b)
                if not last:
                    x1_transposes(b + 1, (1,))
                if b:
                    z_transposes(b - 1)
                    up(b - 1, 2, (3,))
                    if last:
                        lora_up(b - 1, 0)
                        lora_up(b - 1, 1)
                        lora_up(b - 1, 2)
                    out_projection(b)
                if b == 0:
                    x1_transposes(1, (2,))
                    mod_rows("sb", (2, 3))
                    x1_transposes(1, (3,))
                elif not last:
                    x1_transposes(b + 1, (2, 3))
                if last:
                    up(b - 1, 3)
                    lora_up(b - 1, 3)
                elif b:
                    lora_up(b - 1, 0)
                    lora_up(b - 1, 1)
                    lora_up(b - 1, 2)
                    qkv(b + 1, range(NK))
                else:
                    qkv(1, (0, 1))
                    out_projection(0)
                    w_up_transposes((0, 1))
                    mod_rows("cb")
                    qkv(1, (2, 3))
                    mod_columns("sb")
                    mod_columns("cb")
                    mod_rows("gb")
                if b + 1 < B:
                    x2_transposes(b, range(NK))
                    if b == 0:
                        w_up_transposes((2, 3))
                    if b:
                        up(b - 1, 3)
                        lora_up(b - 1, 3)
                    scores(b + 1)
                    v_transposes(b + 1)
            b = B - 1
            x2_transposes_of_tile(0)
            keep_warm(open_bank("x2T", b, 3), 3)
            x2_transposes_of_tile(1)
            keep_warm(at("x2T", b, 3), 6)
            x2_transposes_of_tile(2)
            gate_and_lora_a_of_tile(0)
            x2_transposes_of_tile(3)
            up(b, 0)
            gate_and_lora_a_of_tile(1)
            up(b, 1, (0, 1))
            gate_and_lora_a_of_tile(2)
            gate_and_lora_a_of_tile(3)
            up(b, 1, (2, 3))
            z_to_tokens(b)
            up(b, 2)
            up(b, 3, (0,))
            z_transposes(b)
            up(b, 3, (1,))
            lora_up(b, 0)
            lora_up(b, 1)
            lora_up(b, 2)
            up(b, 3, (2, 3))
            lora_up(b, 3)

        @block.scalar
        def _(act):
            def h1_evacuate(b, kts):
                for kt in kts:
                    act.wait_ge(S["x1T_psum"], NK * b + kt + 1)
                    if b == 0 and kt == 0:
                        act.wait_ge(S["modT_ready"], 2)
                    if b >= 2 and kt == 0:
                        act.wait_ge(S["h1_lo"], NK * b)
                    nc.scalar.activation(h1_full_at[b][:, kt, :], at("x1T", b, kt)[:], ACT.Identity,
                                         bias=modT["sa"][:, kt, b:b + 1], scale=modT["ca"][:, kt, b:b + 1]
                                         ).then_inc(S["h1_full"], 1)

            def h1_high(b, kts):
                for kt in kts:
                    act.wait_ge(S["h1_full"], NK * b + kt + 1)
                    if b and kt == 0:
                        act.wait_ge(S["O_psum"], b)
                    nc.scalar.activation(ahi[:, kt, :], h1_full_at[b][:, kt, :], ACT.Copy).then_inc(S["h1_hi"], 1)

            def ln2_normalise(b):
                for t in range(NT):
                    if b + 1 == B and t >= 2:
                        last_h2_tile(t - 2)
                    act.wait_ge(S["ln2_shift"], NT * b + t + 1)
                    nc.scalar.activation(xn2_p[:, t, :], xs[:, b, t, :], ACT.Identity, bias=shift[:, t:t + 1],
                                         scale=rstd[:, 1, t:t + 1]).then_inc(S["xn2_ready"], 1)
                if b + 1 == B:
                    last_h2_tile(2)
                    last_h2_tile(3)

            def last_h2_tile(t):
                b = B - 1
                q = slice(t * P, (t + 1) * P)
                act.wait_ge(S["x2T_psum"], NK * b + t + 1)
                if t == 0:
                    act.wait_ge(S["h2_lo"], NK * b)
                for kt in range(NK):
                    nc.scalar.activation(h2_full_at[b][:, kt, q], at("x2T", b, t)[:, kt * P:(kt + 1) * P], ACT.Identity,
                                         bias=modT["sb"][:, kt, b:b + 1], scale=modT["cb"][:, kt, b:b + 1]
                                         ).then_inc(S["h2_full"], 1)

            def mod_high(s, kts=range(NK)):
                n = MOD_ORDER.index(s)
                for kt in kts:
                    if s in first_mod_in:
                        act.wait_ge(first_mod_in[s][kt], 16)
                    elif kt == 0:
                        act.wait_ge(mod_in[s], 16)
                    if n >= 2:
                        act.wait_ge(S["mod_kt"], NK * (n - 1 if n > 2 else 0) + kt + 1)
                    nc.scalar.activation(mod_split[s][0][:, kt, :], raw[s][:, kt, :], ACT.Copy).then_inc(S["mod_hi"], 1)

            def qkv_evacuate(b):
                for j in range(2):
                    act.wait_ge(S["qkv_psum"], 3 * b + j + 1)
                    if b:
                        act.wait_ge(S["S_psum"], NT * b)
                    if b == 0 and j == 0:
                        act.wait_ge(small_in, 16)
                    nc.scalar.activation(qk_hi[:, j, :], at("qkv", b, j)[:], ACT.Identity,
                                         bias=bqkv_col[:, j:j + 1]).then_inc(S["qk_hi_ready"], 1)
                act.wait_ge(S["qkv_psum"], 3 * b + 3)
                if b:
                    act.wait_ge(S["V_psum"], b)
                nc.scalar.activation(vT[:], at("qkv", b, 2)[:], ACT.Identity,
                                     bias=bqkv_col[:, 2:3]).then_inc(S["vT_ready"], 1)

            def v_evacuate(b):
                act.wait_ge(S["V_psum"], b + 1)
                nc.scalar.activation(v_hi[:].rearrange("p t d -> p (t d)"), at("V", b)[:],
                                     ACT.Copy).then_inc(S["v_hi_ready"], 1)

            def softmax(b):
                for t in range(NT):
                    if t == NT - 1:
                        v_evacuate(b)
                    act.wait_ge(S["negmax_ready"], NT * b + t + 1)
                    if b and t == 0:
                        act.wait_ge(S["x2T_psum"], NK * b)
                    nc.scalar.activation(xn2_p[:, t, :], at("S", b, t)[:], ACT.Exp, bias=neg_max[:, t:t + 1],
                                         scale=SCORE_SCALE, accum_out=row_sum[:, t:t + 1]).then_inc(S["p_ready"], 1)

            def pt_hi(b, tiles):
                for t in tiles:
                    act.wait_ge(S["PT_psum"], NT * b + t + 1)
                    nc.scalar.activation(ahi[:, :, t * P:(t + 1) * P],
                                         at("PT", b, t)[:].rearrange("p (k q) -> p k q", k=NT),
                                         ACT.Copy).then_inc(S["pt_hi"], 1)

            def h2_evacuate(b):
                for kt in range(NK):
                    n = NK * b + kt
                    act.wait_ge(S["x2T_psum"], n + 1)
                    if b == 0 and kt == 0:
                        act.wait_ge(S["modT_ready"], 4)
                    if b and kt == 0:
                        act.wait_ge(S["h2_lo"], NK * b)
                    nc.scalar.activation(h2_full_at[b][:, kt, :], at("x2T", b, kt)[:], ACT.Identity,
                                         bias=modT["sb"][:, kt, b:b + 1], scale=modT["cb"][:, kt, b:b + 1]
                                         ).then_inc(S["h2_full"], 1)

            def h2_high(b):
                for kt in range(NK):
                    act.wait_ge(S["h2_full"], NK * b + kt + 1)
                    if b and kt == 0:
                        act.wait_ge(S["F_psum"], NT * b)
                    nc.scalar.activation(h2hi[:, kt, :], h2_full_at[b][:, kt, :], ACT.Copy).then_inc(S["h2_hi"], 1)

            def wo_split(b):
                act.wait_ge(S["wo_ga_ready"], b + 1)
                if b:
                    act.wait_ge(S["Y_psum"], NT * b)
                nc.scalar.activation(wo_hi[:], wo_ga[:], ACT.Copy).then_inc(S["wo_hi_ready"], 1)

            def mod_row_evacuate(s):
                n = MOD_ORDER.index(s)
                act.wait_ge(S["mod_kt"], NK * (n + 1))
                if s in MODT:
                    i = MODT.index(s)
                    if i >= 2:
                        act.wait_ge(S["modT_psum"], i - 1)
                    to, rows = mod_row[:, i % 2, :], 2 * B
                else:
                    if s == "gb":
                        act.wait_ge(S["gates_ready"], 1)
                    to, rows = gate_tmp[:, 0, :], B
                nc.scalar.activation(to, at("mod", s)[0:rows, :], ACT.Copy).then_inc(S["mod_row_ready"], 1)

            def gz_evacuate(b):
                act.wait_ge(S["gz_psum"], b + 1)
                if b:
                    act.wait_ge(S["zl_psum"], b)
                nc.scalar.activation(gz[:], at("gz", b)[0:2 * GZ, :], ACT.Copy).then_inc(S["gz_ready"], 1)

            def zT_evacuate(b):
                act.wait_ge(S["zT_psum"], b + 1)
                if b:
                    act.wait_ge(S["F_psum"], NT * b)
                nc.scalar.activation(zT[:], at("zT", b)[:], ACT.Copy).then_inc(S["zT_ready"], 1)

            def wup_high(kts):
                for kt in kts:
                    act.wait_ge(S["wupT_psum"], kt + 1)
                    if kt == NK - 1:
                        act.wait_ge(S["lbw_ready"], 2)
                    nc.scalar.activation(wup_hi[:, kt, :], at("wupT", kt)[:], ACT.Copy).then_inc(S["wup_hi_ready"], 1)

            act.wait_ge(S["cT_psum"], 1)
            nc.scalar.activation(silu_tmp[:, 0, :], at("cT")[:, 0:NK * B], ACT.Exp, scale=-1.0).then_inc(S["silu_step"], 1)
            mod_high("sa")
            mod_high("ca")
            mod_row_evacuate("sa")
            mod_row_evacuate("ca")
            for kt in range(NK):
                act.wait_ge(wqkv_in[kt], 16)
                nc.scalar.activation(wqkv_hi[:, kt, :], raw["wqkv"][:, kt, 0:3 * D], ACT.Copy).then_inc(S["wqkv_hi_ready"], 1)
            for kt in range(NK):
                h1_evacuate(0, (kt,))
                h1_high(0, (kt,))
            mod_high("ga")
            qkv_evacuate(0)
            mod_row_evacuate("ga")
            mod_high("sb", (0, 1))
            softmax(0)
            for b in range(B):
                if b:
                    gz_evacuate(b - 1)
                    pt_hi(b, range(NT))
                    wo_split(b)
                else:
                    pt_hi(b, range(NT))
                    act.wait_ge(S["gateA_psum"], 1)
                    nc.scalar.activation(gzw[:, :, 0, :], at("gateA")[:, 0:NK * GZ].rearrange("p (k g) -> p k g", k=NK),
                                         ACT.Copy).then_inc(S["gzw_hi_ready"], 1)
                    act.wait_ge(S["loraB_psum"], 1)
                    nc.scalar.activation(lb_hi, at("loraB")[:], ACT.Copy).then_inc(S["lb_hi_ready"], 1)
                    mod_high("sb", (2, 3))
                if b + 1 < B:
                    h1_evacuate(b + 1, (0,))
                act.wait_ge(S["O_psum"], b + 1)
                nc.scalar.activation(o_hi[:], at("O", b)[:], ACT.Copy).then_inc(S["o_hi_ready"], 1)
                if b:
                    zT_evacuate(b - 1)
                if b + 1 < B:
                    h1_evacuate(b + 1, (1,))
                    h1_high(b + 1, (0, 1))
                    if b == 0:
                        wo_split(0)
                    for kt in (2, 3):
                        h1_evacuate(b + 1, (kt,))
                        h1_high(b + 1, (kt,))
                if b == 0:
                    mod_row_evacuate("sb")
                    mod_high("cb")
                    wup_high((0, 1))
                    mod_row_evacuate("cb")
                    mod_high("gb")
                ln2_normalise(b)
                if b + 1 < B:
                    qkv_evacuate(b + 1)
                    if b == 0:
                        mod_row_evacuate("gb")
                    h2_evacuate(b)
                    if b == 0:
                        wup_high((2, 3))
                    h2_high(b)
                    softmax(b + 1)
            gz_evacuate(B - 1)
            zT_evacuate(B - 1)

        @block.vector
        def _(dve):
            def ln1_stats(b, tiles):
                for t in tiles:
                    if b == 0:
                        dve.wait_ge(x0_in[t], 16)
                    elif t == 0:
                        dve.wait_ge(x_in[b], 16)
                        dve.wait_ge(S["xn1_ready"], NT * b)
                    nc.vector.bn_stats(stats[:, 0, t, :], xs[:, b, t, :]).then_inc(S["ln1_stats"], 1)

            def ln1_moments(b):
                for t in range(NT):
                    dve.wait_ge(S["ln1_stats"], NT * b + t + 1)
                    nc.vector.bn_aggr(moments[:, 0, t, :], stats[:, 0, t, :]).then_inc(S["ln1_aggr"], 1)
                dve.wait_ge(S["ln1_aggr"], NT * (b + 1))
                nc.vector.tensor_scalar(var_eps[:, 0, :], moments[:, 0, :, 1], LN_EPS, None,
                                        ALU.add).then_inc(S["ln1_var"], 1)

            def first_ln1_aggregate(t):
                dve.wait_ge(S["ln1_stats"], t + 1)
                nc.vector.bn_aggr(moments[:, 0, t, :], stats[:, 0, t, :]).then_inc(S["ln1_aggr"], 1)

            def first_ln1_variance(t):
                dve.wait_ge(S["ln1_aggr"], t + 1)
                nc.vector.tensor_scalar(var_eps[:, 0, t:t + 1], moments[:, 0, t, 1:2], LN_EPS, None,
                                        ALU.add).then_inc(S["ln1_var"], 1)

            def first_ln1():
                ln1_stats(0, (0, 1))
                first_ln1_aggregate(0)
                first_ln1_variance(0)
                ln1_stats(0, (2,))
                first_ln1_aggregate(1)
                first_ln1_variance(1)
                ln1_normalise(0, (0,))
                ln1_stats(0, (3,))
                first_ln1_aggregate(2)
                first_ln1_variance(2)
                first_ln1_aggregate(3)
                first_ln1_variance(3)
                ln1_normalise(0, (1, 2, 3))

            def ln1_normalise(b, tiles=range(NT)):
                if b:
                    dve.wait_ge(S["x1T_psum"], NK * b)
                for t in tiles:
                    dve.wait_ge(S["ln1_rstd"], NT + b if b else t + 1)
                    nc.vector.tensor_scalar(xn1[:, t, :], xs[:, b, t, :], moments[:, 0, t, 0:1], rstd[:, 0, t:t + 1],
                                            ALU.subtract, ALU.mult).then_inc(S["xn1_ready"], 1)

            def mod_low(s, kts):
                n = MOD_ORDER.index(s)
                for kt in kts:
                    dve.wait_ge(S["mod_hi"], NK * n + kt + 1)
                    nc.vector.tensor_tensor(mod_split[s][1][:, kt, :], raw[s][:, kt, :],
                                            mod_split[s][0][:, kt, :].bitcast(F32), ALU.subtract).then_inc(S["mod_lo_dve"], 1)

            def mod_evacuate(s):
                n = MODT.index(s)
                dve.wait_ge(S["modT_psum"], n + 1)
                nc.vector.tensor_reduce(mod_sum[:].rearrange("p (k b) -> p k b", k=NK),
                                        at("modT", s)[:, 0:NK * 2 * B].rearrange("p (k a b) -> p k b a", k=NK, a=2),
                                        AX_X, ALU.add).then_inc(S["mod_sum_ready"], 1)
                dve.wait_ge(S["mod_sum_ready"], n + 1)
                nc.vector.tensor_scalar(modT[s][:].rearrange("p k b -> p (k b)"), mod_sum[:],
                                        1.0 if s in ("ca", "cb") else 0.0, None, ALU.add).then_inc(S["modT_ready"], 1)
                dve.wait_ge(S["modT_ready"], n + 1)

            def gate_rows(i, s):
                dve.wait_ge(S["mod_row_ready"], MOD_ORDER.index(s) + 1)
                nc.vector.scalar_tensor_tensor(gate_tmp[:, 1, :], gate_tmp[:, 0, :], -1.0, gate_tmp[:, 0, :], ALU.mult,
                                               ALU.max).then_inc(S["gate_step"], 1)
                nc.vector.tensor_scalar(gate_tmp[:, 2, :], gate_tmp[:, 0, :], 0.0, 2.0, ALU.is_ge,
                                        ALU.mult).then_inc(S["gate_step"], 1)
                dve.wait_ge(S["gate_step"], GATE_STEPS * i + 2)
                nc.vector.tensor_scalar(gate_tmp[:, 0, :], gate_tmp[:, 1, :], GATE_FLOOR, None,
                                        ALU.max).then_inc(S["gate_step"], 1)
                dve.wait_ge(S["gate_step"], GATE_STEPS * (i + 1))
                nc.vector.scalar_tensor_tensor(gates[:, i, :], gate_tmp[:, 2, :], -1.0, gate_tmp[:, 0, :], ALU.add,
                                               ALU.mult).then_inc(S["gates_ready"], 1)
                dve.wait_ge(S["gates_ready"], i + 1)

            def qk_low(b):
                for j in range(2):
                    dve.wait_ge(S["qk_hi_ready"], 2 * b + j + 1)
                    nc.vector.scalar_tensor_tensor(qk_lo[:, j, :], at("qkv", b, j)[:], bqkv_col[:, j:j + 1],
                                                   qk_hi[:, j, :].bitcast(F32), ALU.add,
                                                   ALU.subtract).then_inc(S["qk_lo_ready"], 1)

            def v_low(b):
                dve.wait_ge(S["v_hi_ready"], b + 1)
                nc.vector.tensor_tensor(v_lo[:].rearrange("p t d -> p (t d)"), at("V", b)[:],
                                        v_hi[:].bitcast(F32).rearrange("p t d -> p (t d)"),
                                        ALU.subtract).then_inc(S["v_lo_ready"], 1)

            def maxima(b):
                for t in range(NT):
                    dve.wait_ge(S["S_psum"], NT * b + t + 1)
                    nc.vector.reduce_max(row_max[:, t:t + 1], at("S", b, t)[:], AX_X).then_inc(S["max_ready"], 1)
                    dve.wait_ge(S["max_ready"], NT * b + t + 1)
                    nc.vector.tensor_scalar(neg_max[:, t:t + 1], row_max[:, t:t + 1], -SCORE_SCALE, None,
                                            ALU.mult).then_inc(S["negmax_ready"], 1)

            def pt_low(b, t):
                dve.wait_ge(S["pt_hi"], NT * b + t + 1)
                q = slice(t * P, (t + 1) * P)
                nc.vector.tensor_tensor(alo[:, :, q], at("PT", b, t)[:].rearrange("p (k q) -> p k q", k=NT),
                                        ahi[:, :, q].bitcast(F32), ALU.subtract).then_inc(S["pt_lo"], 1)

            def inverse_sums(b):
                dve.wait_ge(S["p_ready"], NT * (b + 1))
                nc.vector.reciprocal(row_inv[:], row_sum[:]).then_inc(S["inv_ready"], 1)

            def o_low(b):
                dve.wait_ge(S["o_hi_ready"], b + 1)
                nc.vector.tensor_tensor(o_lo[:], at("O", b)[:], o_hi[:].bitcast(F32),
                                        ALU.subtract).then_inc(S["o_lo_ready"], 1)

            def attention_residual_and_ln2(b):
                dve.wait_ge(S["inv_ready"], b + 1)
                if b:
                    dve.wait_ge(S["ln2_shift"], NT * b)

                def residual(t):
                    dve.wait_ge(S["Y_psum"], NT * b + t + 1)
                    dve.wait_ge(S["xb_ready"], NT * b + t + 1)
                    nc.vector.scalar_tensor_tensor(xs[:, b, t, :], at("Y", b, t)[:], row_inv[:, t:t + 1],
                                                   xs[:, b, t, :], ALU.mult, ALU.add).then_inc(S["x2_ready"], 1)

                for t in range(NT if b + 1 < B else 1):
                    residual(t)
                for t in range(NT):
                    dve.wait_ge(S["x2_ready"], NT * b + t + 1)
                    nc.vector.bn_stats(stats[:, 1, t, :], xs[:, b, t, :]).then_inc(S["ln2_stats"], 1)
                    if b + 1 == B and t + 1 < NT:
                        residual(t + 1)
                    dve.wait_ge(S["ln2_stats"], NT * b + t + 1)
                    nc.vector.bn_aggr(moments[:, 1, t, :], stats[:, 1, t, :]).then_inc(S["ln2_aggr"], 1)
                    dve.wait_ge(S["ln2_aggr"], NT * b + t + 1)
                    nc.vector.tensor_scalar(var_eps[:, 1, t:t + 1], moments[:, 1, t, 1:2], LN_EPS, None,
                                            ALU.add).then_inc(S["ln2_var"], 1)

            def add_parts(b):
                parts = at("zl", b)[:, 0:NT * 2 * GZ].rearrange("p (t a g) -> p t a g", t=NT, a=2)
                done = Z_STEPS * b
                dve.wait_ge(S["zl_psum"], b + 1)
                if b == 0:
                    dve.wait_ge(eb_in, 16 * NT)
                nc.vector.tensor_tensor(zl_tmp[:], parts[:, :, 1, :], logit_bias[:], ALU.add).then_inc(S["z_step"], 1)
                dve.wait_ge(S["z_step"], done + 1)
                nc.vector.tensor_tensor(zl[:], parts[:, :, 0, :], zl_tmp[:], ALU.add).then_inc(S["z_step"], 1)

            def choose_expert(b):
                done = Z_STEPS * b
                dve.wait_ge(S["z_step"], done + 2)
                nc.vector.reduce_max(z_max[:, 0, :], zl[:, :, 0:E], AX_X).then_inc(S["z_step"], 1)
                dve.wait_ge(S["z_step"], done + 3)
                nc.vector.tensor_tensor(z_arg[:, 0], zl[:, :, 0:E], z_max[:, 0, :].unsqueeze(2).to_broadcast([P, NT, E]),
                                        ALU.is_equal).then_inc(S["z_step"], 1)
                dve.wait_ge(S["z_step"], done + 4)
                nc.vector.tensor_tensor(z_arg[:, 1], z_arg[:, 0], first_wins[:], ALU.mult).then_inc(S["z_step"], 1)
                dve.wait_ge(S["z_step"], done + 5)
                nc.vector.reduce_max(z_max[:, 1, :], z_arg[:, 1], AX_X).then_inc(S["z_step"], 1)
                dve.wait_ge(S["z_step"], done + 6)
                nc.vector.tensor_tensor(z_arg[:, 2], z_arg[:, 1], z_max[:, 1, :].unsqueeze(2).to_broadcast([P, NT, E]),
                                        ALU.is_equal).then_inc(S["z_step"], 1)
                dve.wait_ge(S["z_step"], done + 7)
                nc.vector.tensor_tensor(zm[:].rearrange("p t (e r) -> p t e r", e=E),
                                        zl[:, :, E:GZ].rearrange("p t (e r) -> p t e r", e=E),
                                        z_arg[:, 2].unsqueeze(3).to_broadcast([P, NT, E, R]),
                                        ALU.mult).then_inc(S["z_step"], 1)
                dve.wait_ge(S["z_step"], done + 8)
                if b:
                    dve.wait_ge(S["zT_psum"], b)
                twice = zm[:].unsqueeze(2).to_broadcast([P, NT, 2, ER])
                nc.vector.tensor_copy(zst[:, :, :, 0, :], twice).then_inc(S["zst_ready"], 1)
                dve.wait_ge(S["zst_ready"], 2 * b + 1)
                nc.vector.tensor_tensor(zst[:, :, :, 1, :], twice, zst[:, :, :, 0, :].bitcast(F32),
                                        ALU.subtract).then_inc(S["zst_ready"], 1)

            def gate_ffn(b, t):
                n = NT * b + t
                dve.wait_ge(S["F_psum"], n + 1)
                if t == 0:
                    dve.wait_ge(gb_bc_in[b % 2], 16 * (b // 2 + 1))
                if n >= 2 and b + 1 < B:
                    dve.wait_ge(S["out_ready"], n - 1)
                nc.vector.tensor_tensor(gated(n), at("F", b, t)[:], gb_bc[:, b % 2, :],
                                        ALU.mult).then_inc(S["f_gb_ready"], 1)

            def wup_low(kts):
                for kt in kts:
                    dve.wait_ge(S["wup_hi_ready"], kt + 1)
                    nc.vector.tensor_tensor(wup_lo[:, kt, :], at("wupT", kt)[:], wup_hi[:, kt, :].bitcast(F32),
                                            ALU.subtract).then_inc(S["wup_lo_ready"], 1)

            def h1_low(b, kts=range(NK)):
                for kt in kts:
                    dve.wait_ge(S["h1_hi"], NK * b + kt + 1)
                    nc.vector.tensor_tensor(alo[:, kt, :], h1_full_at[b][:, kt, :], ahi[:, kt, :].bitcast(F32),
                                            ALU.subtract).then_inc(S["h1_lo"], 1)

            nc.vector.memset(neg_half[:], -0.5).then_inc(S["dve_const"], 1)
            for e in range(E):
                nc.vector.memset(first_wins[:, :, e], float(E - e)).then_inc(S["dve_const"], 1)
            nc.vector.memset(logit_bias[:], 0.0).then_inc(S["dve_const"], 1)
            dve.wait_ge(S["silu_step"], 1)
            nc.vector.tensor_scalar(silu_tmp[:, 1, :], silu_tmp[:, 0, :], 1.0, None, ALU.add).then_inc(S["silu_step"], 1)
            dve.wait_ge(S["silu_step"], 2)
            nc.vector.reciprocal(silu_tmp[:, 2, :], silu_tmp[:, 1, :]).then_inc(S["silu_step"], 1)
            dve.wait_ge(S["silu_step"], 3)
            nc.vector.tensor_tensor(silu_tmp[:, 0, :], at("cT")[:, 0:NK * B], silu_tmp[:, 2, :], ALU.mult).then_inc(S["silu_step"], 1)
            silu = silu_tmp[:, 0, :].rearrange("p (k b) -> p k b", k=NK)
            dve.wait_ge(S["silu_step"], 4)
            nc.vector.tensor_copy(silu_split[:, :, 0, :], silu).then_inc(S["silu_step"], 1)
            dve.wait_ge(S["silu_step"], 5)
            nc.vector.tensor_tensor(silu_split[:, :, 1, :], silu, silu_split[:, :, 0, :].bitcast(F32),
                                    ALU.subtract).then_inc(S["silu_step"], 1)
            mod_low("sa", (1, 3))
            mod_low("ca", (1, 2, 3))
            first_ln1()
            mod_evacuate("sa")
            mod_evacuate("ca")
            for kt in range(NK):
                h1_low(0, (kt,))
                ln1_stats(1, (kt,))
            ln1_moments(1)
            mod_low("ga", (1, 3))
            dve.wait_ge(lora_b_in, 16 * E)
            for a in range(4):
                nc.vector.tensor_copy(lora_b_rep[:, :, a, :], lora_b_raw[:]).then_inc(S["loraB_rep_ready"], 1)
            ln1_normalise(1, (0, 1))
            dve.wait_ge(small_in, 16)
            qk_low(0)
            maxima(0)
            gate_rows(0, "ga")
            v_low(0)
            for b in range(B):
                if 1 <= b < B - 1:
                    ln1_normalise(b + 1)
                pt_low(b, 0)
                if b == 0:
                    ln1_normalise(1, (2, 3))
                pt_low(b, 1)
                pt_low(b, 2)
                pt_low(b, 3)
                if b:
                    add_parts(b - 1)
                    choose_expert(b - 1)
                else:
                    dve.wait_ge(S["gzw_hi_ready"], 1)
                    nc.vector.tensor_tensor(gzw[:, :, 1, :], at("gateA")[:, 0:NK * GZ].rearrange("p (k g) -> p k g", k=NK),
                                            gzw[:, :, 0, :].bitcast(F32), ALU.subtract).then_inc(S["gzw_lo_ready"], 1)
                    dve.wait_ge(S["lb_hi_ready"], 1)
                    nc.vector.tensor_copy(lbw[0:2 * ER, :], lb_hi[0:2 * ER, :].bitcast(F32)).then_inc(S["lbw_ready"], 1)
                    nc.vector.tensor_tensor(lbw[2 * ER:4 * ER, :], at("loraB")[2 * ER:4 * ER, :],
                                            lb_hi[2 * ER:4 * ER, :].bitcast(F32), ALU.subtract).then_inc(S["lbw_ready"], 1)
                    mod_low("sb", (2, 3))
                inverse_sums(b)
                o_low(b)
                if b == 0:
                    h1_low(1)
                    mod_low("cb", (1, 3))
                if b + 1 == B:
                    gate_ffn(b - 1, 0)
                    gate_ffn(b - 1, 1)
                attention_residual_and_ln2(b)
                if b:
                    if b + 1 < B:
                        gate_ffn(b - 1, 0)
                        gate_ffn(b - 1, 1)
                    gate_ffn(b - 1, 2)
                else:
                    wup_low((0, 1))
                    mod_low("gb", (1, 3))
                    mod_evacuate("sb")
                    mod_evacuate("cb")
                    qk_low(1)
                    gate_rows(1, "gb")
                    wup_low((2, 3))
                if b + 2 < B:
                    ln1_stats(b + 2, (0, 1))
                if b + 1 < B:
                    if b:
                        qk_low(b + 1)
                        gate_ffn(b - 1, 3)
                    maxima(b + 1)
                    if b + 2 < B:
                        ln1_stats(b + 2, (2, 3))
                        ln1_moments(b + 2)
                    v_low(b + 1)
                else:
                    for t in range(NT):
                        q = slice(t * P, (t + 1) * P)
                        dve.wait_ge(S["h2_full"], NK * b + NK * (t + 1))
                        if t == 0:
                            dve.wait_ge(S["F_psum"], NT * b)
                        nc.vector.tensor_copy(h2hi[:, :, q], h2_full_at[b][:, :, q]).then_inc(S["h2_hi"], 1)
                        dve.wait_ge(S["h2_hi"], NK * b + t + 1)
                        nc.vector.tensor_tensor(h2lo[:, :, q], h2_full_at[b][:, :, q], h2hi[:, :, q].bitcast(F32),
                                                ALU.subtract).then_inc(S["h2_lo"], 1)
                        if t == 0:
                            gate_ffn(b - 1, 3)
            add_parts(B - 1)
            choose_expert(B - 1)
            gate_ffn(B - 1, 0)
            gate_ffn(B - 1, 1)
            for t in (2, 3):
                gate_ffn(B - 1, t)
                n = NT * (B - 1) + t
                dve.wait_ge(S["f_gb_ready"], n + 1)
                nc.vector.tensor_tensor(xs[:, B - 1, t, :], xs[:, B - 1, t, :], gated(n), ALU.add).then_inc(last_out_ready, 1)

        @block.gpsimd
        def _(pool):
            def ln1_deviation(b):
                pool.wait_ge(S["ln1_var"], NT + b)
                nc.gpsimd.tensor_tensor(rstd[:, 0, :], var_eps[:, 0, :], neg_half[:], ALU.pow).then_inc(S["ln1_rstd"], 1)

            def first_ln1_deviation(t):
                pool.wait_ge(S["ln1_var"], t + 1)
                if t == 0:
                    pool.wait_ge(S["dve_const"], 1)
                nc.gpsimd.tensor_tensor(rstd[:, 0, t:t + 1], var_eps[:, 0, t:t + 1], neg_half[:, 0:1],
                                        ALU.pow).then_inc(S["ln1_rstd"], 1)

            def output_weights(b):
                pool.wait_ge(ga_bc_in[b % 2], 16 * (b // 2 + 1))
                if b == 0:
                    pool.wait_ge(wo_in, 16)
                    pool.wait_ge(bo_in, 16)
                else:
                    pool.wait_ge(S["wo_hi_ready"], b)
                    pool.wait_ge(S["wo_lo_ready"], b)
                nc.gpsimd.tensor_tensor(wo_ga[:], wo_raw[:], ga_bc[:, b % 2, :], ALU.mult).then_inc(S["wo_ga_ready"], 1)
                if b:
                    pool.wait_ge(S["xb_ready"], NT * b)
                nc.gpsimd.tensor_tensor(gabo[:], bo_bc[:], ga_bc[:, b % 2, :], ALU.mult).then_inc(S["gabo_ready"], 1)

            def split_output_weights(b):
                pool.wait_ge(S["wo_hi_ready"], b + 1)
                nc.gpsimd.tensor_tensor(wo_lo[:], wo_ga[:], wo_hi[:].bitcast(F32), ALU.subtract).then_inc(S["wo_lo_ready"], 1)

            def add_output_bias(b, tiles=range(NT)):
                pool.wait_ge(S["gabo_ready"], b + 1)
                pool.wait_ge(S["xn1_ready"], NT * (b + 1))
                for t in tiles:
                    nc.gpsimd.tensor_tensor(xs[:, b, t, :], xs[:, b, t, :], gabo[:], ALU.add).then_inc(S["xb_ready"], 1)

            def ln2_deviation(b, tiles):
                for t in tiles:
                    n = NT * b + t + 1
                    pool.wait_ge(S["ln2_var"], n)
                    if b:
                        pool.wait_ge(S["xn2_ready"], NT * b)
                    nc.gpsimd.tensor_tensor(rstd[:, 1, t:t + 1], var_eps[:, 1, t:t + 1], neg_half[:, 0:1],
                                            ALU.pow).then_inc(S["ln2_rstd"], 1)
                    pool.wait_ge(S["ln2_rstd"], n)
                    nc.gpsimd.tensor_scalar(shift[:, t:t + 1], moments[:, 1, t, 0:1], rstd[:, 1, t:t + 1], -1.0,
                                            ALU.mult, ALU.mult).then_inc(S["ln2_shift"], 1)

            def mod_low(s, kts=None):
                n = MOD_ORDER.index(s)
                for kt in BY_POOL[s] if kts is None else kts:
                    pool.wait_ge(S["mod_hi"], NK * n + kt + 1)
                    nc.gpsimd.tensor_tensor(mod_split[s][1][:, kt, :], raw[s][:, kt, :],
                                            mod_split[s][0][:, kt, :].bitcast(F32), ALU.subtract).then_inc(S["mod_lo_pool"], 1)

            def h1_low(b, kts):
                for kt in kts:
                    n = NK * b + kt
                    pool.wait_ge(S["h1_hi"], n + 1)
                    nc.gpsimd.tensor_tensor(alo[:, kt, :], h1_full_at[b][:, kt, :], ahi[:, kt, :].bitcast(F32),
                                            ALU.subtract).then_inc(S["h1_lo"], 1)

            def h2_low(b):
                for kt in range(NK):
                    n = NK * b + kt
                    pool.wait_ge(S["h2_hi"], n + 1)
                    nc.gpsimd.tensor_tensor(h2lo[:, kt, :], h2_full_at[b][:, kt, :], h2hi[:, kt, :].bitcast(F32),
                                            ALU.subtract).then_inc(S["h2_lo"], 1)

            def outputs(b, tiles):
                for t in tiles:
                    n = NT * b + t
                    pool.wait_ge(S["f_gb_ready"], n + 1)
                    nc.gpsimd.tensor_tensor(xs[:, b, t, :], xs[:, b, t, :], gated(n), ALU.add).then_inc(S["out_ready"], 1)

            nc.gpsimd.memset(ident[:], 0.0).then_inc(S["const_ready"], 1)
            pool.wait_ge(S["const_ready"], 1)
            nc.gpsimd.affine_select(out=ident[:], in_=ident[:], compare_op=ALU.not_equal, fill=1.0, base=0,
                                    pattern=[[-1, P]], channel_multiplier=1).then_inc(S["const_ready"], 1)

            def wqkv_low(kt):
                pool.wait_ge(S["wqkv_hi_ready"], kt + 1)
                nc.gpsimd.tensor_tensor(wqkv_lo[:, kt, :], raw["wqkv"][:, kt, 0:3 * D], wqkv_hi[:, kt, :].bitcast(F32),
                                        ALU.subtract).then_inc(S["wqkv_lo_ready"], 1)

            mod_low("sa")
            mod_low("ca")
            for t in range(NT):
                first_ln1_deviation(t)
            for kt in range(NK):
                wqkv_low(kt)
            mod_low("ga", (0,))
            ln1_deviation(1)
            mod_low("ga", (2,))
            mod_low("sb")
            for b in range(B):
                output_weights(b)
                if b:
                    add_output_bias(b, (0, 1))
                    split_output_weights(b)
                    add_output_bias(b, (2, 3))
                    if b + 1 < B:
                        h1_low(b + 1, (0, 1, 2))
                        ln2_deviation(b, (0, 1))
                        h1_low(b + 1, (3,))
                        ln2_deviation(b, (2, 3))
                        outputs(b - 1, (0, 1, 2))
                    else:
                        outputs(b - 1, (0, 1))
                        ln2_deviation(b, range(NT))
                        outputs(b - 1, (2, 3))
                else:
                    split_output_weights(b)
                    add_output_bias(b, (0, 1))
                    mod_low("cb", (0,))
                    add_output_bias(b, (2, 3))
                    mod_low("cb", (2,))
                    ln2_deviation(b, range(NT))
                    mod_low("gb")
                if b + 1 < B:
                    h2_low(b)
                    if b:
                        outputs(b - 1, (NT - 1,))
                if b + 2 < B:
                    ln1_deviation(b + 2)
            outputs(B - 1, (0, 1))


_INS = ["L0_attn_x", "L0_attn_Wqkv", "L0_attn_bqkv", "L0_attn_Wo", "L0_attn_bo", "L0_ffn_W_up", "L0_ffn_gate_w",
        "L0_ffn_expert_bias", "L0_ffn_lora_A", "L0_ffn_lora_B", "L0_c", "L0_wmod"]


def kernel(**inputs):
    import numpy as _np
    import concourse.bacc as _bacc
    from concourse.bass_utils import run_bass_kernel_spmd as _run

    nc = _bacc.Bacc("TRN2", target_bir_lowering=False, num_devices=1)
    arrays, args = {}, []
    for name in _INS:
        a = _np.ascontiguousarray(inputs[name])
        arrays[f"in_{name}_dram"] = a
        args.append(nc.dram_tensor(f"in_{name}_dram", a.shape, mybir.dt.from_np(a.dtype), kind="ExternalInput").ap())
    out = nc.dram_tensor("out_0_dram", (B, T, H), F32, kind="ExternalOutput").ap()
    adaln_block(nc, *args, out)
    r = _run(nc, [arrays], core_ids=[0])
    return r.results[0]["out_0_dram"]
```
